# Optimizing a Trainium2 kernel written in Bass

```python
import numpy as np
import jax
import jax.numpy as jnp

def _softmax(x, axis=-1):
    return jax.nn.softmax(x, axis=axis)

def _gelu(x):
    return jax.nn.gelu(x, approximate=True)

def _silu(x):
    return jax.nn.silu(x)

def _sigmoid(x):
    return jax.nn.sigmoid(x)

def _layernorm(x, axis=-1, eps=1e-05):
    m = jnp.mean(x, axis=axis, keepdims=True)
    v = jnp.var(x, axis=axis, keepdims=True)
    return (x - m) / jnp.sqrt(v + eps)

def _scatter_add(tgt, idx, src, axis=0):
    return tgt.at[idx].add(src)

def _segment_sum(src, seg, n):
    return jax.ops.segment_sum(src, seg, n)
kernel_name = 'mk_gnn_resnorm_d2_gnn_r64_521795'

def setup_inputs(seed: int=0):
    np.random.seed(seed)
    _w = jnp.asarray

    def _rec_inputs():
        import jax
        import jax.numpy as jnp
        _gk = jax.random.key(seed)
        x = -0.0003713 + 1 * jax.random.normal(jax.random.fold_in(_gk, 1), (50000, 128), jnp.float32)
        src = jax.random.randint(jax.random.fold_in(_gk, 2), (12500,), 0, 50000, jnp.int32)
        dst = jax.random.randint(jax.random.fold_in(_gk, 3), (12500,), 0, 50000, jnp.int32)
        _o = jnp.argsort(dst, stable=True)
        src = src[_o]
        dst = dst[_o]
        edge_attr_64 = jax.random.uniform(jax.random.fold_in(_gk, 12), (12500, 64), jnp.float32, 0.0, 1)
        edge_weight = jax.random.uniform(jax.random.fold_in(_gk, 14), (12500,), jnp.float32, 0.0, 1)
        return (x, src, dst, edge_attr_64, edge_weight)
    x, src, dst, edge_attr_64, edge_weight = _rec_inputs()

    def _L0_gnn_setup():
        import jax, jax.numpy as jnp
        import numpy as np
        N_NODES = 100000
        D = 128
        N_EDGES = 25000
        NUM_LAYERS = 3
        key = jax.random.key(seed)
        k1, k2, k3, k4 = jax.random.split(key, 4)
        ebds = jax.random.normal(k1, (N_NODES, D), dtype=jnp.float32)
        edge_val = jax.random.uniform(k2, (N_EDGES,), dtype=jnp.float32)
        edge_row = jax.random.randint(k3, (N_EDGES,), 0, N_NODES, dtype=jnp.int32)
        edge_col = jax.random.randint(k4, (N_EDGES,), 0, N_NODES, dtype=jnp.int32)
        return {'ebds': ebds, 'edge_val': edge_val, 'edge_row': edge_row, 'edge_col': edge_col, 'num_layers': NUM_LAYERS}
    _L0_gnn_all = _L0_gnn_setup()
    _L0_gnn_in = {k: v for k, v in _L0_gnn_all.items() if k in ()}
    del _L0_gnn_all

    def _L1_gnn_setup():
        import jax, jax.numpy as jnp
        import numpy as np
        N_ATOMS = 50000
        N_PAIRS = 12500
        F = 128
        R = 64
        N_RES = 3
        key = jax.random.key(seed)
        ks = jax.random.split(key, 16)
        s = 1.0 / np.sqrt(F)
        inp = {'atomic_embedding': jax.random.normal(ks[0], (N_ATOMS, F), jnp.float32), 'f_ij': jax.random.uniform(ks[1], (N_PAIRS, R), jnp.float32), 'pair_indices': jax.random.randint(ks[2], (2, N_PAIRS), 0, N_ATOMS, jnp.int64) if jax.config.jax_enable_x64 else jax.random.randint(ks[2], (2, N_PAIRS), 0, N_ATOMS, jnp.int32), 'Wg': jax.random.normal(ks[3], (F, R), jnp.float32) / np.sqrt(R), 'Wi': jax.random.normal(ks[4], (F, F), jnp.float32) * s, 'bi': jnp.zeros((F,), jnp.float32), 'Wj': jax.random.normal(ks[5], (F, F), jnp.float32) * s, 'bj': jnp.zeros((F,), jnp.float32), 'Wv': jax.random.normal(ks[6], (F, F), jnp.float32) * s, 'bv': jnp.zeros((F,), jnp.float32), 'gate': jnp.ones((F,), jnp.float32), 'res_W1': jax.random.normal(ks[7], (N_RES, F, F), jnp.float32) * s, 'res_b1': jnp.zeros((N_RES, F), jnp.float32), 'res_W2': jax.random.normal(ks[8], (N_RES, F, F), jnp.float32) * s, 'res_b2': jnp.zeros((N_RES, F), jnp.float32)}
        return inp
    _L1_gnn_all = _L1_gnn_setup()
    _L1_gnn_in = {k: v for k, v in _L1_gnn_all.items() if k in ('Wg', 'Wi', 'bi', 'Wj', 'bj', 'Wv', 'bv', 'gate', 'res_W1', 'res_b1', 'res_W2', 'res_b2')}
    del _L1_gnn_all
    return {'x': x, 'src': src, 'dst': dst, 'edge_attr_64': edge_attr_64, 'edge_weight': edge_weight, 'L1_gnn_Wg': _L1_gnn_in['Wg'], 'L1_gnn_Wi': _L1_gnn_in['Wi'], 'L1_gnn_bi': _L1_gnn_in['bi'], 'L1_gnn_Wj': _L1_gnn_in['Wj'], 'L1_gnn_bj': _L1_gnn_in['bj'], 'L1_gnn_Wv': _L1_gnn_in['Wv'], 'L1_gnn_bv': _L1_gnn_in['bv'], 'L1_gnn_gate': _L1_gnn_in['gate'], 'L1_gnn_res_W1': _L1_gnn_in['res_W1'], 'L1_gnn_res_b1': _L1_gnn_in['res_b1'], 'L1_gnn_res_W2': _L1_gnn_in['res_W2'], 'L1_gnn_res_b2': _L1_gnn_in['res_b2']}

def reference(x, src, dst, edge_attr_64, edge_weight, L1_gnn_Wg, L1_gnn_Wi, L1_gnn_bi, L1_gnn_Wj, L1_gnn_bj, L1_gnn_Wv, L1_gnn_bv, L1_gnn_gate, L1_gnn_res_W1, L1_gnn_res_b1, L1_gnn_res_W2, L1_gnn_res_b2):
    import jax
    import jax.numpy as jnp

    def _L0_gnn_ref(ebds, edge_val, edge_row, edge_col, num_layers):
        import jax, jax.numpy as jnp
        import numpy as np
        N_NODES = 100000
        D = 128
        N_EDGES = 25000
        NUM_LAYERS = 3
        'LightGCN forward: repeated SpMM with running layer-sum.\n\n            adj is COO: out[r] += val[e] * x[c] for each edge e=(r,c).\n            Equivalent to torch.spmm(adj, x) applied num_layers times,\n            summing all layer outputs (including layer 0 input).\n            '
        n = ebds.shape[0]

        def spmm(x):
            msgs = edge_val[:, None] * x[edge_col]
            return jax.ops.segment_sum(msgs, edge_row, num_segments=n)
        acc = ebds
        cur = ebds
        for _ in range(num_layers):
            cur = spmm(cur)
            acc = acc + cur
        return acc

    def _L1_gnn_ref(atomic_embedding, f_ij, pair_indices, Wg, Wi, bi, Wj, bj, Wv, bv, gate, res_W1, res_b1, res_W2, res_b2):
        import jax, jax.numpy as jnp
        import numpy as np
        N_ATOMS = 50000
        N_PAIRS = 12500
        F = 128
        R = 64
        N_RES = 3
        sp = jax.nn.softplus
        idx_i = pair_indices[0]
        idx_j = pair_indices[1]
        x = sp(atomic_embedding)
        g = f_ij @ Wg.T
        u = sp(x @ Wi.T + bi)
        msg = sp(x[idx_j] @ Wj.T + bj) * g
        u = u + jax.ops.segment_sum(msg, idx_i, num_segments=x.shape[0])
        for k in range(res_W1.shape[0]):
            h = sp(sp(u) @ res_W1[k].T + res_b1[k])
            u = u + h @ res_W2[k].T + res_b2[k]
        u = sp(u)
        return gate * x + u @ Wv.T + bv
    edge_index = jnp.stack([src, dst])
    x = _layernorm(x + _L0_gnn_ref(x, edge_weight, src, dst, 3), axis=-1)
    x = _layernorm(x + _L1_gnn_ref(x, edge_attr_64, edge_index, L1_gnn_Wg, L1_gnn_Wi, L1_gnn_bi, L1_gnn_Wj, L1_gnn_bj, L1_gnn_Wv, L1_gnn_bv, L1_gnn_gate, L1_gnn_res_W1, L1_gnn_res_b1, L1_gnn_res_W2, L1_gnn_res_b2), axis=-1)
    return x

_drawn_inputs = setup_inputs


def setup_inputs(seed=0):
    import zlib

    import numpy as np

    out = dict(_drawn_inputs(seed))
    spreads = {'L1_gnn_bi': (0.0, 0.566),
     'L1_gnn_bj': (0.0, 2.0),
     'L1_gnn_bv': (0.0, 0.1),
     'L1_gnn_gate': (1.0, 0.2),
     'L1_gnn_res_b1': (0.0, 0.294),
     'L1_gnn_res_b2': (0.0, 0.1)}
    factors = {}
    for name, (base, spread) in spreads.items():
        noise = np.random.default_rng([zlib.crc32(name.encode()), seed]).standard_normal(out[name].shape)
        drawn = base * np.exp(spread * noise) if base else spread * noise
        out[name] = jnp.asarray(drawn.astype(out[name].dtype))
    for name, factor in factors.items():
        out[name] = (out[name] * factor).astype(out[name].dtype)
    return out
```

```python
from contextlib import ExitStack

import concourse.bass as bass
from concourse import mybir

ALU = mybir.AluOpType
ACT = mybir.ActivationFunctionType
F32 = mybir.dt.float32
BF16 = mybir.dt.bfloat16
I32 = mybir.dt.int32

P = 128
TPG = 4
GW = TPG * P
DIG = 256
CHAINS = 4
CAP = 2.0 ** 63
EPS = 1e-05
FAR = 100000.0


def plan(n_groups):
    runs, full = [], n_groups // CHAINS
    if full:
        runs.append((full, CHAINS, 0))
    if n_groups % CHAINS:
        runs.append((1, n_groups % CHAINS, full * CHAINS))
    return runs


def gnn_kernel(nc, x, src, dst, attr, weight, Wg, Wi, bi, Wj, bj, Wv, bv, gate, W1, b1, W2, b2, out):
    N, F = x.shape
    E, R = attr.shape
    RES = W1.shape[0]
    assert F == P and N < DIG * DIG and RES == 3
    ET = -(-E // GW) * TPG
    EP = ET * P
    EG = ET // TPG
    FULLT, TAIL = E // P, E % P
    NG = -(-N // GW)
    ZROW = EP
    PW = 4 + R

    def dram(name, shape, dt):
        return nc.dram_tensor(name, shape, dt, kind="Internal").ap()

    ptr_table = dram("ptr_table", (2 * P * DIG, 1), I32)
    sorted_rows = dram("sorted_rows", (EP, PW), F32)
    sorted_src = dram("sorted_src", (ET, P), F32)
    totals = [dram(f"totals{k}", (EP + 1, F), F32) for k in range(3)]

    with ExitStack() as ctx:
        def sb(name, shape, dt=F32):
            return ctx.enter_context(nc.sbuf_tensor(name, shape, dt))

        def sem(name):
            return ctx.enter_context(nc.semaphore(name))

        bank = ctx.enter_context(nc.psum_tensor("bank", [P, 8, GW], F32))

        ident = sb("ident", [P, P])
        ones = sb("ones", [P, P])
        digits = sb("digits", [P, DIG], BF16)
        hi_no = sb("hi_no", [P, 2])
        ones_bf = sb("ones_bf", [P, P], BF16)
        zero_row = sb("zero_row", [1, P])
        mats = {"Wi": Wi, "Wj": Wj, "Wv": Wv}
        for k in range(RES):
            mats[f"W1_{k}"] = W1[k]
            mats[f"W2_{k}"] = W2[k]
        order = list(mats)
        carry_mask = sb("carry_mask", [P, EP], BF16)
        setup_space, at_s = carry_mask[:].bitcast(F32), [0]

        def carve_s(shape, dt=F32):
            words = shape[1] * (shape[2] if len(shape) > 2 else 1)
            v = setup_space[0:shape[0], at_s[0]:at_s[0] + words]
            at_s[0] += words
            v = v if dt == F32 else v.bitcast(dt)
            return v.rearrange("p (a b) -> p a b", b=shape[2]) if len(shape) > 2 else v

        below = carve_s([P, P])
        pick_last = carve_s([P, P])
        shift_up = carve_s([P, P])
        wrap = carve_s([P, P])
        col_minus_row = carve_s([P, P])
        row_no = carve_s([P, P])
        earlier = carve_s([P, P])
        w_nat = carve_s([P, len(order), P])
        wT = sb("wT", [P, len(order), P])
        wg_nat = carve_s([P, 2, P])
        wgT = sb("wgT", [P, 2, P])
        gate_diag = sb("gate_diag", [P, P])
        cols = sb("cols", [P, 16])
        C_BI, C_GATE, C_B1, C_B2, C_SUM = 0, 1, 2, 2 + RES, 2 + 2 * RES
        brow = sb("brow", [1, 2, 3, P])
        bpart = sb("bpart", [1, 2, 3, TPG, P], BF16)
        bias3 = sb("bias3", [3, 2, GW], BF16)
        row_buf = sb("row_buf", [P, EP])
        M_buf = sb("M_buf", [P, EP])
        G = sb("G", [P, EP])
        rows_nat = carve_s([P, 2, P], I32)
        w_rows = carve_s([P, P])
        rows_f = carve_s([P, 4, P])
        rows_i = carve_s([P, 2, P], I32)
        e_cols = carve_s([P, 5, ET])
        dst_idx = sb("dst_idx", [P, ET], I32)
        pos = sb("pos", [P, ET])
        pos_idx = sb("pos_idx", [P, ET], I32)
        meta = sb("meta", [P, ET, 4])
        src_s = sb("src_s", [P, ET + 1])
        w_s = sb("w_s", [P, ET])
        prev_last = sb("prev_last", [P, ET])
        same_next = sb("same_next", [P, ET])
        srcT = sb("srcT", [P, P])
        node_idx = sb("node_idx", [P, ET], I32)
        out_idx = sb("out_idx", [P, ET], I32)
        src_rows = row_buf[:].bitcast(I32)
        payload = M_buf[:, 0:ET * PW].rearrange("p (t w) -> p t w", w=PW)
        payload_i = M_buf[:, 0:ET * PW].bitcast(I32).rearrange("p (t w) -> p t w", w=PW)
        meta_i = meta[:].rearrange("p t w -> p (t w)").bitcast(I32).rearrange("p (t w) -> p t w", w=4)

        at = [0]

        def carve(words, dt=F32):
            v = G[:, at[0]:at[0] + words]
            at[0] += words
            return v if dt == F32 else v.bitcast(dt)

        oh_hi = [carve(DIG // 2, BF16) for _ in range(TPG)]
        oh_lo = [carve(DIG // 2, BF16) for _ in range(TPG)]
        hi_row = carve(GW, I32)
        oh_hiT = [carve(GW) for _ in range(2)]
        same = carve(P)
        junk = carve(DIG)
        acc_a, acc_b = carve(TPG), carve(TPG)
        cum = [carve(2 * DIG) for _ in range(2)]
        hist, incl, base, ptr_f = (carve(2 * DIG) for _ in range(4))
        zeros = carve(DIG)
        offs = carve(2)
        ptr_i = carve(2 * DIG, I32)

        seg_m = [sb(f"seg_m{h}", [P, 2 * P]) for h in range(2)]
        seg_T = [sb(f"seg_T{h}", [P, 2 * P]) for h in range(2)]

        at_m = [0]

        def carve_m(words):
            v = M_buf[:, at_m[0]:at_m[0] + words]
            at_m[0] += words
            return v

        X, X1, S, EL, H = ([carve_m(GW) for _ in range(CHAINS)] for _ in range(5))
        attr_in = [carve_m(TPG * R) for _ in range(CHAINS)]
        attrT = [H[c][:, 0:2 * P] for c in range(CHAINS)]
        zeros_w = carve_s([P, P])
        zeros_r = carve_s([P, GW])
        tick = sb("tick", [P, 1])
        seg_M = [carve_m(2 * P) for _ in range(2)]
        stats = [sb(f"stats{c}", [P, TPG, 6]) for c in range(CHAINS)]
        mv = [sb(f"mv{c}", [P, 2, TPG, 2]) for c in range(CHAINS)]
        ve = [sb(f"ve{c}", [P, 2, TPG]) for c in range(CHAINS)]
        rs = [sb(f"rs{c}", [P, 2, TPG]) for c in range(CHAINS)]
        nm = [sb(f"nm{c}", [P, TPG]) for c in range(CHAINS)]
        minus_half = sb("minus_half", [P, TPG])

        iotas, consts = sem("iotas"), sem("consts")
        w_loaded, b_loaded = sem("w_loaded"), sem("b_loaded")
        wT_psum, wT_ready = sem("wT_psum"), sem("wT_ready")
        bias_parts, bias_ready = sem("bias_parts"), sem("bias_ready")
        pads_set, rows_loaded, row_bcast = sem("pads_set"), sem("rows_loaded"), sem("row_bcast")
        pads_attr, attr_loaded = sem("pads_attr"), sem("attr_loaded")
        rows_split, cols_psum, cols_ready = sem("rows_split"), sem("cols_psum"), sem("cols_ready")
        idx_ready = sem("idx_ready")
        onehot_ready, hist_added = sem("onehot_ready"), sem("hist_added")
        scan_ready, offs_psum, ptr_ready, ptr_stored = sem("scan_ready"), sem("offs_psum"), sem("ptr_ready"), sem("ptr_stored")
        tile_onehots, onehotT_ready = sem("tile_onehots"), sem("onehotT_ready")
        cum_copied, cum_added, place_psum, place_read = sem("cum_copied"), sem("cum_added"), sem("place_psum"), sem("place_read")
        pos_ready, ptr_gathered, payload_set, scattered = sem("pos_ready"), sem("ptr_gathered"), sem("payload_set"), sem("scattered")
        meta_loaded, meta_split, near_psum, near_ready = sem("meta_loaded"), sem("meta_split"), sem("near_psum"), sem("near_ready")
        srcT_stored, srow_loaded, masks_ready = sem("srcT_stored"), sem("srow_loaded"), sem("masks_ready")
        zero_stored = sem("zero_stored")
        xd_gathered = sem("xd_gathered")
        tot_gathered = [sem(f"tot_gathered{k}") for k in range(3)]
        seg_in, seg_mm, seg_fixed, seg_tr, seg_rows = sem("seg_in"), sem("seg_mm"), sem("seg_fixed"), sem("seg_tr"), sem("seg_rows")
        seg_mask = sem("seg_mask")
        tot_stored = sem("tot_stored")
        srow_again, xs_gathered = sem("srow_again"), sem("xs_gathered")
        chain, link_sem, place_link = sem("carry_chain"), sem("link"), sem("place_link")
        srcT_ready, wg_zeroed = sem("srcT_ready"), sem("wg_zeroed")

        def chain_sems(pre):
            return {k: sem(f"{pre}_{k}") for k in
                    ("v", "stats", "mean", "var", "rstd", "x1", "xT", "exp_s", "s", "lin", "exp", "capped", "log", "sp",
                     "y", "ysum", "nmean", "o", "u0", "attrT", "attr_copied", "g", "msg")}

        ms, ns = chain_sems("msg"), chain_sems("node")
        attr_arrived = [sem(f"attr_arrived{c}") for c in range(CHAINS)]
        x_arrived = [sem(f"x_arrived{c}") for c in range(CHAINS)]
        out_stored = [sem(f"out_stored{c}") for c in range(CHAINS)]

        def runs_of(kinds):
            runs, before, used = [], 0, [0] * CHAINS
            for kind, count in kinds:
                for reps, n, first in plan(count):
                    runs.append((kind, reps, n, first, before, list(used)))
                    before += reps * n
                    for c in range(n):
                        used[c] += reps
            return runs, used

        msg_runs, _ = runs_of([("msg", EG)])
        node_runs, node_used = runs_of([("node", NG), ("edge", EG)])

        def each_run(eng, runs, body):
            for kind, reps, n, first, before, used in runs:
                if reps > 1:
                    with eng.Fori(0, reps) as g:
                        body(kind, n, g * n + first, g * n + before, [g + u for u in used])
                else:
                    body(kind, n, first, before, used)

        def nth(per, before, n, k, c):
            return before * per + (k * n + c + 1)

        block = ctx.enter_context(nc.Block())

        @block.sync
        def _(sp):
            for i, name in enumerate(order):
                sp.dma_start(w_nat[:, i, :], mats[name]).then_inc(w_loaded, 16)
            sp.wait_ge(wg_zeroed, 1)
            for i in range(2):
                sp.dma_start(wg_nat[:, i, i * R:(i + 1) * R], Wg).then_inc(w_loaded, 16)
            with nc.allow_non_contiguous_dma(reason="small columns"):
                for v, at_c in [(bi, C_BI), (gate, C_GATE)] + [(b1[k], C_B1 + k) for k in range(RES)] + [(b2[k], C_B2 + k) for k in range(RES)]:
                    sp.dma_start(cols[:, at_c:at_c + 1], v.rearrange("(p o) -> p o", o=1)).then_inc(b_loaded, 16)
            sp.dma_start(brow[:, 0, 0, :], bv.rearrange("(o f) -> o f", o=1)).then_inc(b_loaded, 16)
            sp.dma_start(brow[:, 1, 0, :], bj.rearrange("(o f) -> o f", o=1)).then_inc(b_loaded, 16)

            sp.wait_ge(pads_set, 5)
            for v, rows in ((src, rows_nat[:, 0, :]), (dst, rows_nat[:, 1, :]), (weight, w_rows[:])):
                sp.dma_start(rows[0:FULLT, :], v[0:FULLT * P].rearrange("(t p) -> t p", p=P)).then_inc(rows_loaded, 16)
                sp.dma_start(rows[FULLT:FULLT + 1, 0:TAIL], v[FULLT * P:E].rearrange("(o p) -> o p", o=1)).then_inc(rows_loaded, 16)
            sp.dma_start(src_rows[:, 0:E], src.rearrange("(o e) -> o e", o=1).to_broadcast([P, E])).then_inc(row_bcast, 16)
            sp.dma_start(payload[:, 0:FULLT, 4:PW], attr[0:FULLT * P].rearrange("(t p) f -> p t f", p=P)).then_inc(attr_loaded, 16)
            sp.dma_start(payload[0:TAIL, FULLT, 4:PW], attr[FULLT * P:E]).then_inc(attr_loaded, 16)
            sp.wait_ge(consts, 1)
            for k in range(3):
                sp.dma_start(totals[k][ZROW:ZROW + 1, :], zero_row[:]).then_inc(zero_stored, 16)
            sp.wait_ge(bias_parts, 1)
            for part in range(3):
                for q in range(2):
                    sp.dma_start(bias3[part:part + 1, q, :], bpart[:, q, part, :, :].rearrange("o a b -> o (a b)")).then_inc(bias_ready, 16)

            sp.wait_ge(ptr_ready, 1)
            sp.dma_start(ptr_table.rearrange("(c p l) o -> p c (l o)", c=2, l=DIG), ptr_i.rearrange("p (c l) -> p c l", c=2)).then_inc(ptr_stored, 16)

            sp.wait_ge(scattered, 16 * ET)
            with nc.allow_non_contiguous_dma(reason="four words of each row"):
                sp.dma_start(meta[:], sorted_rows.rearrange("(t p) w -> p t w", p=P)[:, :, 0:4]).then_inc(meta_loaded, 16)
            sp.wait_ge(srcT_ready, 1)
            sp.dma_start(sorted_src, srcT[0:ET, :]).then_inc(srcT_stored, 16)
            sp.wait_ge(srcT_stored, 16)
            sp.dma_start(row_buf[:], sorted_src.rearrange("t p -> (t p)").rearrange("(o e) -> o e", o=1).to_broadcast([P, EP])).then_inc(srow_loaded, 16)

            for k in range(3):
                with sp.Fori(0, EG) as g:
                    sp.wait_ge(seg_rows, (g + EG * k) * 2 + 2)
                    sp.dma_start(totals[k][bass.ds(g * GW, GW), :].rearrange("(j p) f -> p j f", p=P),
                                 G[:, bass.ds(g * GW, GW)].rearrange("p (j f) -> p j f", f=F)).then_inc(tot_stored, 16)

            def attr_loads(kind, n, grp, before, used):
                sp.wait_ge(ms["attrT"], before)
                for c in range(n):
                    sp.dma_start(attr_in[c].rearrange("p (j r) -> p j r", r=R),
                                 sorted_rows[bass.ds((grp + c) * GW, GW), :].rearrange("(j p) w -> p j w", p=P)[:, :, 4:PW]).then_inc(attr_arrived[c], 16)

            sp.wait_ge(seg_mm, 2 * EG * 3)
            each_run(sp, msg_runs, attr_loads)

            sp.wait_ge(ms["v"], EG)
            sp.dma_start(row_buf[:], sorted_src.rearrange("t p -> (t p)").rearrange("(o e) -> o e", o=1).to_broadcast([P, EP])).then_inc(srow_again, 16)

            def node_loads(kind, n, grp, before, used):
                sp.wait_ge(ns["x1"], before)
                for c in range(n):
                    Xc = X[c].rearrange("p (j f) -> p j f", f=F)
                    if kind == "node":
                        row = (grp + c) * GW if not isinstance(grp, int) else min((grp + c) * GW, N - GW)
                        sp.dma_start(Xc, x[bass.ds(row, GW), :].rearrange("(p j) f -> p j f", j=TPG)).then_inc(x_arrived[c], 16)
                    else:
                        sp.dma_start(Xc, totals[2][bass.ds((grp + c) * GW, GW), :].rearrange("(j p) f -> p j f", p=P)).then_inc(x_arrived[c], 16)

            sp.wait_ge(ms["x1"], EG)
            each_run(sp, node_runs, node_loads)

        @block.gpsimd
        def _(pool):
            exact = dict(allow_small_or_imprecise_dtypes=True)
            pool.iota(col_minus_row[:], [[1, P]], base=0, channel_multiplier=-1, **exact).then_inc(iotas, 1)
            pool.iota(row_no[:], [[0, P]], base=0, channel_multiplier=1, **exact).then_inc(iotas, 1)
            pool.iota(digits[:], [[1, DIG]], base=0, channel_multiplier=0, **exact).then_inc(iotas, 1)
            pool.iota(hi_no[:], [[P, 2]], base=0, channel_multiplier=1, **exact).then_inc(iotas, 1)
            pool.iota(rows_nat[:, 0, :], [[1, P]], base=N - E, channel_multiplier=P).then_inc(pads_set, 1)
            pool.memset(rows_nat[:, 1, :], 0).then_inc(pads_set, 1)
            pool.memset(w_rows[:], 0.0).then_inc(pads_set, 1)
            pool.iota(src_rows[:, E:EP], [[1, EP - E]], base=N, channel_multiplier=0).then_inc(pads_set, 1)
            pool.memset(payload[:, FULLT:ET, :], 0.0).then_inc(pads_set, 1)
            pool.memset(minus_half[:], -0.5).then_inc(iotas, 1)

            pool.wait_ge(ptr_stored, 16)
            pool.wait_ge(idx_ready, 1)
            pool.wait_ge(attr_loaded, 32)
            for t in range(ET):
                pool.indirect_dma_start(payload_i[:, t, 2:3], None, ptr_table,
                                        bass.IndirectOffsetOnAxis(ap=dst_idx[:, t:t + 1], axis=0)).then_inc(ptr_gathered, 16)
            pool.wait_ge(ptr_gathered, 16 * ET)
            pool.wait_ge(pos_ready, 1)
            pool.wait_ge(payload_set, 1)
            for t in range(ET):
                pool.indirect_dma_start(sorted_rows, bass.IndirectOffsetOnAxis(ap=pos_idx[:, t:t + 1], axis=0),
                                        payload[:, t, :], None).then_inc(scattered, 16)
            pool.wait_ge(masks_ready, EG)
            for t in range(ET):
                pool.indirect_dma_start(row_buf[:, t * P:(t + 1) * P], None, x,
                                        bass.IndirectOffsetOnAxis(ap=meta_i[:, t, 1:2], axis=0)).then_inc(xd_gathered, 16)
            pool.wait_ge(zero_stored, 48)
            for k in range(3):
                pool.wait_ge(tot_stored, 16 * EG * (k + 1))
                for t in range(ET):
                    pool.indirect_dma_start(G[:, t * P:(t + 1) * P], None, totals[k],
                                            bass.IndirectOffsetOnAxis(ap=meta_i[:, t, 2:3], axis=0)).then_inc(tot_gathered[k], 16)

            def rstd(sems, per, n, before, k):
                for c in range(n):
                    pool.wait_ge(sems["var"], nth(per, before, n, k, c))
                    pool.tensor_tensor(rs[c][:, k, :], ve[c][:, k, :], minus_half[:], ALU.pow).then_inc(sems["rstd"], 1)

            each_run(pool, msg_runs, lambda kind, n, grp, before, used: rstd(ms, 1, n, before, 0))

            pool.wait_ge(seg_in, 2 * EG * 4)
            for t in range(ET):
                pool.indirect_dma_start(row_buf[:, t * P:(t + 1) * P], None, x,
                                        bass.IndirectOffsetOnAxis(ap=node_idx[:, t:t + 1], axis=0)).then_inc(xs_gathered, 16)

            def finish(kind, n, grp, before, used):
                rstd(ns, 2, n, before, 0)
                rstd(ns, 2, n, before, 1)
                for c in range(n):
                    pool.wait_ge(ns["o"], nth(1, before, n, 0, c))
                    if kind == "node":
                        row = (grp + c) * GW if not isinstance(grp, int) else min((grp + c) * GW, N - GW)
                        if isinstance(grp, int) and c and row != (grp + c) * GW:
                            pool.wait_ge(out_stored[c - 1], (used[c - 1] + 1) * 16)
                        pool.dma_start(out[bass.ds(row, GW), :].rearrange("(p j) f -> p j f", j=TPG),
                                       H[c].rearrange("p (j f) -> p j f", f=F)).then_inc(out_stored[c], 16)

            for run in node_runs:
                if run[0] == "node":
                    each_run(pool, [run], finish)
            for c in range(CHAINS):
                pool.wait_ge(out_stored[c], 16 * sum(r[1] for r in node_runs if r[0] == "node" and c < r[2]))
            stores = [16 * sum(r[1] for r in node_runs if r[0] == "node" and c < r[2]) for c in range(CHAINS)]
            for kind, reps, n, first, before, used in [r for r in node_runs if r[0] == "edge"]:
                for g in range(reps):
                    finish(kind, n, first + g * n, before + g * n, None)
                    for c in range(n):
                        for j in range(TPG):
                            t = (first + g * n + c) * TPG + j
                            pool.indirect_dma_start(out, bass.IndirectOffsetOnAxis(ap=out_idx[:, t:t + 1], axis=0),
                                                    H[c][:, j * P:(j + 1) * P], None,
                                                    bounds_check=N - 1, oob_is_err=False).then_inc(out_stored[c], 16)
                            stores[c] += 16
            for c in range(CHAINS):
                pool.wait_ge(out_stored[c], stores[c])

        def act_source(sems, n, before):
            act = nc.scalar
            for c in range(n):
                act.wait_ge(sems["xT"], nth(1, before, n, 0, c))
                act.activation(EL[c], bank[:, 4 + c, :], ACT.Exp).then_inc(sems["exp_s"], 1)
            for c in range(n):
                act.wait_ge(sems["exp_s"], nth(1, before, n, 0, c))
                act.activation(S[c], EL[c], ACT.Ln, bias=1.0).then_inc(sems["s"], 1)

        def act_softplus(sems, per, k, n, before, ready, bank0, bias):
            act = nc.scalar
            for c in range(n):
                ready(act, c)
                if bias is None:
                    act.activation(EL[c], bank[:, bank0 + c, :], ACT.Exp).then_inc(sems["exp"], 1)
                else:
                    act.activation(EL[c], bank[:, bank0 + c, :], ACT.Exp, bias=cols[:, bias:bias + 1]).then_inc(sems["exp"], 1)
            for c in range(n):
                act.wait_ge(sems["capped"], nth(per, before, n, k, c))
                act.activation(EL[c], EL[c], ACT.Ln, bias=1.0).then_inc(sems["log"], 1)

        def act_msg(kind, n, grp, before, used):
            act = nc.scalar
            for c in range(n):
                act.wait_ge(ms["attrT"], nth(1, before, n, 0, c))
                act.copy(attrT[c], bank[:, c, 0:2 * P]).then_inc(ms["attr_copied"], 1)
            act_source(ms, n, before)
            act_softplus(ms, 1, 0, n, before, lambda e, c: e.wait_ge(ms["lin"], nth(1, before, n, 0, c)), 4, None)

        U, HB = 0, 4
        STEPS = [(U, C_BI, None)]
        for r in range(RES):
            STEPS.append((U, C_SUM + r - 1 if r else None, 3 + 2 * r))
            STEPS.append((HB, C_B1 + r, 4 + 2 * r))
        STEPS.append((U, C_SUM + RES - 1, 2))
        NSTEP = len(STEPS)

        def act_node(kind, n, grp, before, used):
            act = nc.scalar
            act_source(ns, n, before)
            for k, (bank0, bias, _) in enumerate(STEPS):
                def ready(e, c):
                    if k == 1:
                        e.wait_ge(ns["sp"], nth(NSTEP, before, n, 0, c))
                    else:
                        e.wait_ge(ns["lin"], nth(NSTEP - 1, before, n, max(k - 1, 0), c))
                act_softplus(ns, NSTEP, k, n, before, ready, bank0, bias)
            for c in range(n):
                act.wait_ge(ns["nmean"], nth(1, before, n, 0, c))
                for j in range(TPG):
                    w = slice(j * P, (j + 1) * P)
                    last = act.activation(H[c][:, w], EL[c][:, w], ACT.Identity, bias=nm[c][:, j:j + 1], scale=rs[c][:, 1, j:j + 1])
                last.then_inc(ns["o"], 1)

        @block.scalar
        def _(act):
            act.wait_ge(wT_psum, 1)
            act.copy(wT[:, 0:TPG, :], bank[:, 0, :].rearrange("p (j f) -> p j f", f=P)).then_inc(wT_ready, 1)
            act.copy(wT[:, TPG:2 * TPG, :], bank[:, 1, :].rearrange("p (j f) -> p j f", f=P)).then_inc(wT_ready, 1)
            act.copy(wT[:, 2 * TPG, :], bank[:, 2, 0:P]).then_inc(wT_ready, 1)
            act.copy(wgT[:], bank[:, 3, 0:2 * P].rearrange("p (i f) -> p i f", f=P)).then_inc(wT_ready, 1)

            with act.Fori(0, EG) as g:
                for j in range(TPG):
                    act.wait_ge(cum_added, g * TPG + j + 1)
                    act.wait_ge(place_psum, g * TPG + max(j - 1, 0) if j else g * TPG)
                    act.copy(cum[j % 2], bank[:, 0, :]).then_inc(cum_copied, 1)

            for k in range(4):
                with act.Fori(0, EG) as g:
                    done = (g + EG * k) * 2
                    for h in range(2):
                        cols_of = bass.ds(g * GW + h * 2 * P, 2 * P)
                        if k < 3:
                            act.wait_ge(seg_tr, done + h + 1)
                            act.copy(G[:, cols_of], bank[:, 2 + h, 0:2 * P]).then_inc(seg_rows, 1)
                        else:
                            act.wait_ge(seg_fixed, done + h + 1)
                            act.copy(G[:, cols_of], seg_T[h][:]).then_inc(seg_rows, 1)
                if k == 2:
                    each_run(act, msg_runs, act_msg)

            each_run(act, node_runs, act_node)

        @block.tensor
        def _(pe):
            pe.wait_ge(consts, 1)
            pe.wait_ge(w_loaded, 16 * (len(order) + 2))
            for i in range(len(order)):
                pe.transpose(bank[:, i // TPG, (i % TPG) * P:(i % TPG + 1) * P], w_nat[:, i, :], ident[:])
            for i in range(2):
                mm = pe.transpose(bank[:, 3, i * P:(i + 1) * P], wg_nat[:, i, :], ident[:])
            mm.then_inc(wT_psum, 1)

            pe.wait_ge(rows_split, 1)
            pe.wait_ge(wT_ready, 4)
            for q in range(4):
                pe.transpose(bank[:, 4, q * P:(q + 1) * P], rows_f[:, q, :], ident[:])
            pe.transpose(bank[:, 5, 0:P], w_rows[:], ident[:]).then_inc(cols_psum, 1)

            pe.matmul(bank[:, 0, :], zeros_w[:], zeros_r[:], start=True, stop=False, skip_group_check=True)
            with pe.Fori(0, EG) as g:
                for j in range(TPG):
                    pe.wait_ge(onehot_ready, g * TPG + j + 1)
                    for c in range(2):
                        mm = pe.matmul(bank[:, 0, c * DIG:(c + 1) * DIG], oh_hi[j][:, c * P:(c + 1) * P], oh_lo[j],
                                       start=False, stop=True, skip_group_check=True)
                    mm.then_inc(hist_added, 1)
            pe.wait_ge(scan_ready, 1)
            pe.matmul(bank[:, 1, 0:1], below[:], incl[:, DIG - 1:DIG], start=True, stop=True)
            pe.matmul(bank[:, 1, 1:2], below[:], incl[:, 2 * DIG - 1:2 * DIG], start=True, stop=False)
            pe.matmul(bank[:, 1, 1:2], ones[:], incl[:, DIG - 1:DIG], start=False, stop=True).then_inc(offs_psum, 1)

            pe.wait_ge(ptr_ready, 1)
            pe.matmul(bank[:, 0, :], ident[:], base, start=True, stop=False, skip_group_check=True).then_inc(cum_added, 1)
            with pe.Fori(0, EG) as g:
                pe.wait_ge(onehotT_ready, g + 1)
                for j in range(TPG):
                    pe.wait_ge(cum_copied, g * TPG + j + 1)
                    pe.wait_ge(tile_onehots, g * TPG + j + 1)
                    for c in range(2):
                        mm = pe.matmul(bank[:, 0, c * DIG:(c + 1) * DIG], oh_hi[j][:, c * P:(c + 1) * P], oh_lo[j],
                                       start=False, stop=True, skip_group_check=True)
                    mm.then_inc(cum_added, 1)
                    pe.wait_ge(place_read, g * TPG + max(j - 1, 0))
                    for c in range(2):
                        mm = pe.matmul(bank[:, 2 + j % 2, 0:DIG], oh_hiT[c][:, j * P:(j + 1) * P], cum[j % 2][:, c * DIG:(c + 1) * DIG],
                                       start=(c == 0), stop=(c == 1))
                    mm.then_inc(place_psum, 1)

            pe.wait_ge(meta_split, 1)
            pe.matmul(bank[:, 4, 0:ET], pick_last[:], src_s[:, 0:ET], start=True, stop=True)
            pe.matmul(bank[:, 4, P:P + ET], shift_up[:], src_s[:, 0:ET], start=True, stop=False, skip_group_check=True)
            pe.matmul(bank[:, 4, P:P + ET], wrap[:], src_s[:, 1:ET + 1], start=False, stop=True, skip_group_check=True)
            pe.transpose(bank[0:ET, 5, 0:P], src_s[:, 0:ET], ident[:]).then_inc(near_psum, 1)

            def segment_products(k):
                with pe.Fori(0, EG) as g:
                    done = (g + EG * k) * 2
                    pe.wait_ge(seg_fixed, done)
                    for h in range(2):
                        pe.wait_ge(seg_in, done + h + 1)
                        for j in range(2):
                            w = slice(j * P, (j + 1) * P)
                            masks = M_buf[:, bass.ds(g * GW + (2 * h + j) * P, P)] if k < 3 else seg_M[h][:, w]
                            mm = pe.matmul(bank[:, h, w], seg_m[h][:, w], masks, start=True, stop=True)
                        mm.then_inc(seg_mm, 1)
                    if k < 3:
                        for h in range(2):
                            pe.wait_ge(seg_fixed, done + h + 1)
                            pe.wait_ge(seg_rows, done)
                            for j in range(2):
                                w = slice(j * P, (j + 1) * P)
                                mm = pe.transpose(bank[:, 2 + h, w], seg_T[h][:, w], ident[:])
                            mm.then_inc(seg_tr, 1)

            def transposes(sems, n, before):
                for c in range(n):
                    pe.wait_ge(sems["x1"], nth(1, before, n, 0, c))
                    for j in range(TPG):
                        w = slice(j * P, (j + 1) * P)
                        mm = pe.transpose(bank[:, HB + c, w], X1[c][:, w], ident[:])
                    mm.then_inc(sems["xT"], 1)

            def pe_msg(kind, n, grp, before, used):
                for c in range(n):
                    pe.wait_ge(attr_arrived[c], (used[c] + 1) * 16)
                    pe.wait_ge(ms["msg"], before)
                    for i in range(2):
                        mm = pe.transpose(bank[:, U + c, i * P:(i + 1) * P], attr_in[c][:, i * P:(i + 1) * P], ident[:])
                    mm.then_inc(ms["attrT"], 1)
                transposes(ms, n, before)
                for c in range(n):
                    pe.wait_ge(ms["attr_copied"], nth(1, before, n, 0, c))
                    for j in range(TPG):
                        w = slice(j * P, (j + 1) * P)
                        mm = pe.matmul(bank[:, U + c, w], attrT[c][:, (j // 2) * P:(j // 2 + 1) * P], wgT[:, j % 2, :], start=True, stop=True)
                    mm.then_inc(ms["g"], 1)
                for c in range(n):
                    pe.wait_ge(ms["s"], nth(1, before, n, 0, c))
                    pe.matmul(bank[:, HB + c, :], ones_bf[0:3, :], bias3[:, 1, :], start=True, stop=False, skip_group_check=True)
                    for j in range(TPG):
                        w = slice(j * P, (j + 1) * P)
                        mm = pe.matmul(bank[:, HB + c, w], S[c][:, w], wT[:, 1, :], start=False, stop=True, skip_group_check=True)
                    mm.then_inc(ms["lin"], 1)

            def pe_node(kind, n, grp, before, used):
                transposes(ns, n, before)
                for c in range(n):
                    pe.wait_ge(ns["s"], nth(1, before, n, 0, c))
                    pe.matmul(bank[:, U + c, :], wT[:, 0, :], S[c], start=True, stop=True, skip_group_check=True).then_inc(ns["lin"], 1)
                for k in range(1, NSTEP - 1):
                    bank0, bias, w_at = STEPS[k]
                    for c in range(n):
                        pe.wait_ge(ns["sp"], nth(NSTEP, before, n, k, c))
                        pe.matmul(bank[:, (HB if bank0 == U else U) + c, :], wT[:, w_at, :], H[c],
                                  start=(bank0 == U), stop=True, skip_group_check=True).then_inc(ns["lin"], 1)
                for c in range(n):
                    pe.wait_ge(ns["sp"], nth(NSTEP, before, n, NSTEP - 1, c))
                    pe.matmul(bank[:, HB + c, :], ones_bf[0:3, :], bias3[:, 0, :], start=True, stop=False, skip_group_check=True)
                    for j in range(TPG):
                        w = slice(j * P, (j + 1) * P)
                        pe.matmul(bank[:, HB + c, w], S[c][:, w], gate_diag[:], start=False, stop=False, skip_group_check=True)
                        mm = pe.matmul(bank[:, HB + c, w], H[c][:, w], wT[:, 2, :], start=False, stop=True, skip_group_check=True)
                    mm.then_inc(ns["y"], 1)

            for k in range(3):
                segment_products(k)
            pe.wait_ge(bias_ready, 96)
            pe.wait_ge(seg_rows, 2 * EG * 3)
            each_run(pe, msg_runs, pe_msg)
            pe.wait_ge(ms["msg"], EG)
            segment_products(3)
            pe.wait_ge(seg_fixed, 2 * EG * 4)
            each_run(pe, node_runs, pe_node)

        @block.vector
        def _(dve):
            links = [0]

            def link(ins):
                links[0] += 1
                ins.then_inc(link_sem, 1)
                dve.wait_ge(link_sem, links[0])

            dve.memset(wg_nat, 0.0).then_inc(wg_zeroed, 1)
            dve.memset(zero_row[:], 0.0)
            dve.memset(ones[:], 1.0)
            dve.memset(ones_bf[:], 1.0)
            dve.memset(zeros_w[:], 0.0)
            dve.memset(zeros_r[:], 0.0)
            dve.memset(seg_T[0][:], 0.0)
            dve.memset(seg_T[1][:], 0.0)
            dve.memset(src_s[:, ET:ET + 1], -1.0)
            dve.memset(prev_last[:, 0:1], -1.0)
            dve.wait_ge(iotas, 5)
            dve.tensor_scalar(ident[:], col_minus_row[:], 0.0, None, ALU.is_equal)
            dve.tensor_scalar(below[:], col_minus_row[:], 0.0, None, ALU.is_gt)
            dve.tensor_scalar(earlier[:], col_minus_row[:], 0.0, None, ALU.is_lt)
            dve.tensor_scalar(shift_up[:], col_minus_row[:], -1.0, None, ALU.is_equal)
            dve.tensor_scalar(pick_last[:], row_no[:], float(P - 1), None, ALU.is_equal)
            link(dve.tensor_scalar(wrap[:], col_minus_row[:], float(P - 1), None, ALU.is_equal))
            dve.wait_ge(b_loaded, 16 * (4 + 2 * RES))
            link(dve.tensor_scalar(gate_diag[:], ident[:], cols[:, C_GATE:C_GATE + 1], None, ALU.mult))
            link(dve.tensor_copy(cols[:, C_SUM:C_SUM + 1], cols[:, C_B2:C_B2 + 1]))
            for k in range(1, RES):
                link(dve.tensor_tensor(cols[:, C_SUM + k:C_SUM + k + 1], cols[:, C_SUM + k - 1:C_SUM + k], cols[:, C_B2 + k:C_B2 + k + 1], ALU.add))
            dve.memset(tick[:], 0.0).then_inc(consts, 1)
            for part in range(3):
                link(dve.tensor_copy(bpart[:, :, part, 0, :], brow[:, :, part, :]))
                if part < 2:
                    link(dve.tensor_tensor(brow[:, :, part + 1, :], brow[:, :, part, :], bpart[:, :, part, 0, :], ALU.subtract))
                for r in range(1, TPG):
                    last = dve.tensor_copy(bpart[:, :, part, r, :], bpart[:, :, part, 0, :])
            last.then_inc(bias_parts, 1)

            dve.wait_ge(rows_loaded, 96)
            dve.tensor_copy(rows_f[:, 0, :], rows_nat[:, 0, :])
            dve.tensor_copy(rows_f[:, 3, :], rows_nat[:, 1, :])
            dve.tensor_scalar(rows_i[:, 0, :], rows_nat[:, 0, :], 8, None, ALU.logical_shift_right)
            link(dve.tensor_scalar(rows_i[:, 1, :], rows_nat[:, 0, :], DIG - 1, None, ALU.bitwise_and))
            dve.tensor_copy(rows_f[:, 1:3, :], rows_i[:, :, :]).then_inc(rows_split, 1)
            dve.wait_ge(cols_psum, 1)
            dve.tensor_copy(e_cols[:, 0:4, :], bank[:, 4, :].rearrange("p (q t) -> p q t", q=4)[:, :, 0:ET])
            link(dve.tensor_copy(e_cols[:, 4, :], bank[:, 5, 0:ET]))
            dve.tensor_copy(dst_idx[:], e_cols[:, 3, :]).then_inc(idx_ready, 1)
            dve.wait_ge(attr_loaded, 32)
            dve.wait_ge(idx_ready, 1)
            dve.tensor_copy(payload[:, :, 0], e_cols[:, 0, :])
            dve.tensor_copy(payload_i[:, :, 1], dst_idx[:])
            dve.tensor_copy(payload[:, :, 3], e_cols[:, 4, :]).then_inc(payload_set, 1)

            with dve.Fori(0, EG) as g:
                dve.wait_ge(hist_added, g * TPG)
                for j in range(TPG):
                    t = bass.ds(g * TPG + j, 1)
                    dve.tensor_scalar(oh_hi[j], digits[:], e_cols[:, 1, t], None, ALU.is_equal)
                    dve.tensor_scalar(oh_lo[j], digits[:], e_cols[:, 2, t], None, ALU.is_equal).then_inc(onehot_ready, 1)
            dve.memset(zeros, 0.0)
            dve.wait_ge(hist_added, ET)
            link(dve.tensor_copy(hist, bank[:, 0, :]))
            for c in range(2):
                w = slice(c * DIG, (c + 1) * DIG)
                last = dve.tensor_tensor_scan(incl[:, w], hist[:, w], zeros, 0.0, ALU.add, ALU.add)
            last.then_inc(scan_ready, 1)
            dve.wait_ge(offs_psum, 1)
            link(dve.tensor_copy(offs, bank[:, 1, 0:2]))
            for c in range(2):
                w = slice(c * DIG, (c + 1) * DIG)
                dve.scalar_tensor_tensor(out=base[:, w], in0=incl[:, w], scalar=offs[:, c:c + 1], in1=hist[:, w], op0=ALU.add, op1=ALU.subtract)
                link(dve.tensor_scalar(ptr_f[:, w], incl[:, w], offs[:, c:c + 1], float(-1 - ZROW), ALU.add, ALU.add))
            link(dve.tensor_scalar(hist, hist, 1.0, None, ALU.min))
            link(dve.tensor_tensor(ptr_f, ptr_f, hist, ALU.mult))
            dve.tensor_scalar(ptr_i, ptr_f, float(ZROW), None, ALU.add).then_inc(ptr_ready, 1)

            dve.wait_ge(row_bcast, 16)
            with dve.Fori(0, EG) as g:
                chunk = bass.ds(g * GW, GW)
                dve.wait_ge(place_psum, g * TPG)
                dve.tensor_scalar(hi_row, src_rows[:, chunk], 8, None, ALU.logical_shift_right).then_inc(place_link, 1)
                dve.wait_ge(place_link, g * (2 + 2 * TPG) + 1)
                dve.tensor_scalar(oh_hiT[0], hi_row, hi_no[:, 0:1], None, ALU.is_equal)
                dve.tensor_scalar(oh_hiT[1], hi_row, hi_no[:, 1:2], None, ALU.is_equal).then_inc(onehotT_ready, 1)
                for j in range(TPG):
                    t = bass.ds(g * TPG + j, 1)
                    dve.tensor_scalar(oh_hi[j], digits[:], e_cols[:, 1, t], None, ALU.is_equal)
                    dve.tensor_scalar(oh_lo[j], digits[:], e_cols[:, 2, t], None, ALU.is_equal).then_inc(tile_onehots, 1)
                for j in range(TPG):
                    t = bass.ds(g * TPG + j, 1)
                    dve.tensor_scalar(same, src_rows[:, bass.ds(g * GW + j * P, P)], e_cols[:, 0, t], None, ALU.is_equal).then_inc(place_link, 1)
                    dve.wait_ge(place_link, g * (2 + 2 * TPG) + 2 + 2 * j)
                    dve.tensor_tensor_reduce(junk[:, 0:P], same, earlier[:], 1.0, 0.0, ALU.mult, ALU.add, acc_b[:, j:j + 1]).then_inc(place_link, 1)
                    dve.wait_ge(place_link, g * (2 + 2 * TPG) + 3 + 2 * j)
                    dve.wait_ge(place_psum, g * TPG + j + 1)
                    last = dve.tensor_tensor_reduce(junk, bank[:, 2 + j % 2, 0:DIG], oh_lo[j], 1.0, 0.0, ALU.mult, ALU.add, acc_a[:, j:j + 1])
                    last.then_inc(place_read, 1)
                dve.wait_ge(place_read, g * TPG + TPG)
                dve.tensor_tensor(pos[:, bass.ds(g * TPG, TPG)], acc_a, acc_b, ALU.add).then_inc(place_link, 1)
                dve.wait_ge(place_link, g * (2 + 2 * TPG) + 2 + 2 * TPG)
            dve.tensor_copy(pos_idx[:], pos[:]).then_inc(pos_ready, 1)

            dve.wait_ge(meta_loaded, 16)
            dve.tensor_copy(w_s[:], meta[:, :, 3])
            dve.tensor_copy(src_s[:, 0:ET], meta[:, :, 0]).then_inc(meta_split, 1)
            dve.wait_ge(near_psum, 1)
            dve.tensor_copy(srcT[0:ET, :], bank[0:ET, 5, 0:P]).then_inc(srcT_ready, 1)
            dve.tensor_copy(prev_last[:, 1:ET], bank[:, 4, 0:ET - 1])
            link(dve.tensor_tensor(same_next[:], src_s[:, 0:ET], bank[:, 4, P:P + ET], ALU.is_equal))
            link(dve.scalar_tensor_tensor(out=pos[:], in0=same_next[:], scalar=FAR, in1=src_s[:, 0:ET], op0=ALU.mult, op1=ALU.add))
            dve.tensor_copy(out_idx[:], pos[:])
            link(dve.tensor_scalar(same_next[:], src_s[:, 0:ET], float(N - 1), None, ALU.min))
            link(dve.tensor_copy(node_idx[:], same_next[:]))
            dve.wait_ge(srow_loaded, 16)
            with dve.Fori(0, EG) as g:
                for j in range(TPG):
                    t = bass.ds(g * TPG + j, 1)
                    tile = bass.ds(g * GW + j * P, P)
                    dve.tensor_scalar(M_buf[:, tile], row_buf[:, tile], src_s[:, t], w_s[:, t], ALU.is_equal, ALU.mult)
                    last = dve.tensor_scalar(carry_mask[:, tile], row_buf[:, tile], prev_last[:, t], None, ALU.is_equal)
                last.then_inc(masks_ready, 1)
            dve.wait_ge(masks_ready, EG)

            def segment_sums(k):
                if k == 0:
                    dve.wait_ge(xd_gathered, 16 * ET)
                elif k < 3:
                    dve.wait_ge(tot_gathered[k - 1], 16 * ET)
                else:
                    dve.wait_ge(srow_again, 16)
                with dve.Fori(0, EG) as g:
                    done = (g + EG * k) * 2
                    for h in range(2):
                        half = bass.ds(g * GW + 2 * h * P, 2 * P)
                        if k == 0:
                            ins = dve.tensor_copy(seg_m[h][:], row_buf[:, half])
                        elif k < 3:
                            ins = dve.tensor_tensor(seg_m[h][:], row_buf[:, half], G[:, half], ALU.add)
                        else:
                            dve.tensor_copy(seg_m[h][:], G[:, half])
                            for j in range(2):
                                ins = dve.tensor_scalar(seg_M[h][:, j * P:(j + 1) * P], row_buf[:, bass.ds(g * GW + (2 * h + j) * P, P)],
                                                        src_s[:, bass.ds(g * TPG + 2 * h + j, 1)], None, ALU.is_equal)
                        ins.then_inc(seg_in, 1)
                    dve.wait_ge(seg_rows, done)
                    for h in range(2):
                        dve.wait_ge(seg_mm, done + h + 1)
                        for j in range(2):
                            i = 2 * h + j
                            before_T = seg_T[1 - h] if j == 0 else seg_T[h]
                            carry = before_T[:, 2 * P - 1:2 * P] if j == 0 else before_T[:, P - 1:P]
                            dve.wait_ge(chain, (g + EG * k) * TPG + i)
                            w = slice(j * P, (j + 1) * P)
                            ins = dve.scalar_tensor_tensor(out=seg_T[h][:, w], in0=carry_mask[:, bass.ds(g * GW + i * P, P)], scalar=carry,
                                                           in1=bank[:, h, w], op0=ALU.mult, op1=ALU.add)
                            ins.then_inc(chain, 1)
                        dve.wait_ge(chain, (g + EG * k) * TPG + 2 * h + 2)
                        dve.memset(tick[:], 0.0).then_inc(seg_fixed, 1)

            def ln_stats(sems, per, k, n, before, src_of, ready):
                for c in range(n):
                    ready(c)
                    for j in range(TPG):
                        last = dve.bn_stats(stats[c][:, j, :], src_of[c][:, j * P:(j + 1) * P])
                    last.then_inc(sems["stats"], 1)
                dve.wait_ge(sems["stats"], nth(per, before, n, k, n - 1))
                dve.memset(tick[:], 0.0)
                for c in range(n):
                    for j in range(TPG):
                        last = dve.bn_aggr(mv[c][:, k, j, :], stats[c][:, j, :])
                    last.then_inc(sems["mean"], 1)
                for c in range(n):
                    dve.wait_ge(sems["mean"], nth(per, before, n, k, c))
                    dve.tensor_scalar(ve[c][:, k, :], mv[c][:, k, :, 1], EPS / 4 if k == 0 else EPS, None, ALU.add).then_inc(sems["var"], 1)

            def normalise(sems, per, n, before):
                for c in range(n):
                    dve.wait_ge(sems["rstd"], nth(per, before, n, 0, c))
                    for j in range(TPG):
                        w = slice(j * P, (j + 1) * P)
                        last = dve.tensor_scalar(X1[c][:, w], X[c][:, w], mv[c][:, 0, j, 0:1], rs[c][:, 0, j:j + 1], ALU.subtract, ALU.mult)
                    last.then_inc(sems["x1"], 1)

            def softplus(sems, per, k, n, before, bank0, bias, to, done="sp"):
                for c in range(n):
                    dve.wait_ge(sems["exp"], nth(per, before, n, k, c))
                    dve.tensor_scalar(EL[c], EL[c], CAP, None, ALU.min).then_inc(sems["capped"], 1)
                for c in range(n):
                    dve.wait_ge(sems["log"], nth(per, before, n, k, c))
                    if bias is None:
                        ins = dve.tensor_tensor(to(c), bank[:, bank0 + c, :], EL[c], ALU.max)
                    else:
                        ins = dve.scalar_tensor_tensor(out=to(c), in0=bank[:, bank0 + c, :], scalar=cols[:, bias:bias + 1], in1=EL[c],
                                                       op0=ALU.add, op1=ALU.max)
                    ins.then_inc(sems[done], 1)

            def dve_msg(kind, n, grp, before, used):
                for c in range(n):
                    rows = bass.ds((grp + c) * GW, GW)
                    dve.scalar_tensor_tensor(out=X[c], in0=G[:, rows], scalar=0.5, in1=row_buf[:, rows], op0=ALU.mult, op1=ALU.add).then_inc(ms["v"], 1)
                ln_stats(ms, 1, 0, n, before, X, lambda c: dve.wait_ge(ms["v"], nth(1, before, n, 0, c)))
                normalise(ms, 1, n, before)
                dve.wait_ge(ms["g"], nth(1, before, n, 0, n - 1))
                softplus(ms, 1, 0, n, before, HB, None, lambda c: H[c])
                for c in range(n):
                    dve.wait_ge(ms["sp"], nth(1, before, n, 0, c))
                    dve.tensor_tensor(G[:, bass.ds((grp + c) * GW, GW)], bank[:, U + c, :], H[c], ALU.mult).then_inc(ms["msg"], 1)

            def dve_node(kind, n, grp, before, used):
                for c in range(n):
                    dve.wait_ge(x_arrived[c], (used[c] + 1) * 16)
                    if kind == "edge":
                        dve.scalar_tensor_tensor(out=X[c], in0=X[c], scalar=0.5, in1=row_buf[:, bass.ds((grp + c) * GW, GW)],
                                                 op0=ALU.mult, op1=ALU.add).then_inc(ns["v"], 1)
                edges_before = before - NG

                def ready(c):
                    if kind == "edge":
                        dve.wait_ge(ns["v"], nth(1, edges_before, n, 0, c))
                ln_stats(ns, 2, 0, n, before, X, ready)
                normalise(ns, 2, n, before)
                for c in range(n):
                    if kind == "node":
                        dve.wait_ge(out_stored[c], used[c] * 16)
                    else:
                        nodes = sum(r[1] for r in node_runs if r[0] == "node" and c < r[2])
                        dve.wait_ge(out_stored[c], (used[c] - nodes) * (16 * TPG) + 16 * nodes)
                for k, (bank0, bias, _) in enumerate(STEPS):
                    if k:
                        softplus(ns, NSTEP, k, n, before, bank0, bias, lambda c: H[c])
                    elif kind == "node":
                        softplus(ns, NSTEP, k, n, before, bank0, bias, lambda c: bank[:, U + c, :])
                    else:
                        softplus(ns, NSTEP, k, n, before, bank0, bias, lambda c: H[c], done="u0")
                        for c in range(n):
                            dve.wait_ge(ns["u0"], nth(1, edges_before, n, 0, c))
                            dve.tensor_tensor(bank[:, U + c, :], H[c], G[:, bass.ds((grp + c) * GW, GW)], ALU.add).then_inc(ns["sp"], 1)
                for c in range(n):
                    dve.wait_ge(ns["y"], nth(1, before, n, 0, c))
                    dve.tensor_tensor(EL[c], bank[:, HB + c, :], X1[c], ALU.add).then_inc(ns["ysum"], 1)
                ln_stats(ns, 2, 1, n, before, EL, lambda c: dve.wait_ge(ns["ysum"], nth(1, before, n, 0, c)))
                for c in range(n):
                    dve.wait_ge(ns["rstd"], nth(2, before, n, 1, c))
                    dve.scalar_tensor_tensor(out=nm[c][:], in0=mv[c][:, 1, :, 0], scalar=-1.0, in1=rs[c][:, 1, :],
                                             op0=ALU.mult, op1=ALU.mult).then_inc(ns["nmean"], 1)

            for k in range(3):
                segment_sums(k)
            dve.wait_ge(tot_gathered[2], 16 * ET)
            dve.wait_ge(seg_mm, 2 * EG * 3)
            each_run(dve, msg_runs, dve_msg)
            dve.wait_ge(ms["msg"], EG)
            segment_sums(3)
            dve.wait_ge(xs_gathered, 16 * ET)
            dve.wait_ge(seg_rows, 2 * EG * 4)
            each_run(dve, node_runs, dve_node)


_INS = ["x", "src", "dst", "edge_attr_64", "edge_weight", "L1_gnn_Wg", "L1_gnn_Wi", "L1_gnn_bi", "L1_gnn_Wj", "L1_gnn_bj",
        "L1_gnn_Wv", "L1_gnn_bv", "L1_gnn_gate", "L1_gnn_res_W1", "L1_gnn_res_b1", "L1_gnn_res_W2", "L1_gnn_res_b2"]


def kernel(**inputs):
    import numpy as _np
    import concourse.bacc as _bacc
    from concourse import mybir as _mybir
    from concourse.bass_utils import run_bass_kernel_spmd as _run

    nc = _bacc.Bacc("TRN2", target_bir_lowering=False, num_devices=1)
    arrays, args = {}, []
    for name in _INS:
        a = _np.ascontiguousarray(inputs[name])
        arrays[f"in_{name}"] = a
        args.append(nc.dram_tensor(f"in_{name}", a.shape, _mybir.dt.from_np(a.dtype), kind="ExternalInput").ap())
    out = nc.dram_tensor("out_0", arrays["in_x"].shape, _mybir.dt.float32, kind="ExternalOutput").ap()
    gnn_kernel(nc, *args, out)
    r = _run(nc, [arrays], core_ids=[0])
    return r.results[0]["out_0"]
```

```python
from contextlib import ExitStack

import concourse.bass as bass
from concourse import mybir

ALU = mybir.AluOpType
ACT = mybir.ActivationFunctionType
F32 = mybir.dt.float32
BF16 = mybir.dt.bfloat16
I32 = mybir.dt.int32

P = 128
TPG = 4
GW = TPG * P
DIG = 256
CHAINS = 4
CAP = 2.0 ** 63
EPS = 1e-05
FAR = 100000.0


def plan(n_groups):
    runs, full = [], n_groups // CHAINS
    if full:
        runs.append((1, CHAINS, 0))
        runs.append((full - 1, CHAINS, CHAINS))
    if n_groups % CHAINS:
        runs.append((1, n_groups % CHAINS, full * CHAINS))
    return runs


def gnn_kernel(nc, x, src, dst, attr, weight, Wg, Wi, bi, Wj, bj, Wv, bv, gate, W1, b1, W2, b2, out):
    N, F = x.shape
    E, R = attr.shape
    RES = W1.shape[0]
    assert F == P and N < DIG * DIG and RES == 3
    ET = -(-E // GW) * TPG
    EP = ET * P
    EG = ET // TPG
    FULLT, TAIL = E // P, E % P
    NG = -(-N // GW)
    ZROW = EP
    PW = 4 + R

    def dram(name, shape, dt):
        return nc.dram_tensor(name, shape, dt, kind="Internal").ap()

    ptr_table = dram("ptr_table", (2 * P * DIG, 1), I32)
    sorted_rows = dram("sorted_rows", (EP, PW), F32)
    sorted_src = dram("sorted_src", (ET, P), F32)
    totals = [dram(f"totals{k}", (EP + 1, F), F32) for k in range(3)]

    with ExitStack() as ctx:
        def sb(name, shape, dt=F32):
            return ctx.enter_context(nc.sbuf_tensor(name, shape, dt))

        def sem(name):
            return ctx.enter_context(nc.semaphore(name))

        bank = ctx.enter_context(nc.psum_tensor("bank", [P, 8, GW], F32))

        ident = sb("ident", [P, P])
        ones = sb("ones", [P, P])
        digits = sb("digits", [P, DIG], BF16)
        hi_no = sb("hi_no", [P, 2])
        ones_bf = sb("ones_bf", [P, P], BF16)
        zero_row = sb("zero_row", [1, P])
        mats = {"Wi": Wi, "Wj": Wj, "Wv": Wv}
        for k in range(RES):
            mats[f"W1_{k}"] = W1[k]
            mats[f"W2_{k}"] = W2[k]
        order = list(mats)
        carry_mask = sb("carry_mask", [P, EP], BF16)
        setup_space, at_s = carry_mask[:].bitcast(F32), [0]

        def carve_s(shape, dt=F32):
            words = shape[1] * (shape[2] if len(shape) > 2 else 1)
            v = setup_space[0:shape[0], at_s[0]:at_s[0] + words]
            at_s[0] += words
            v = v if dt == F32 else v.bitcast(dt)
            return v.rearrange("p (a b) -> p a b", b=shape[2]) if len(shape) > 2 else v

        below = carve_s([P, P])
        pick_last = carve_s([P, P])
        shift_up = carve_s([P, P])
        wrap = carve_s([P, P])
        col_minus_row = carve_s([P, P])
        row_no = carve_s([P, P])
        earlier = carve_s([P, P])
        w_nat = carve_s([P, len(order), P])
        wT = sb("wT", [P, len(order), P])
        wg_nat = carve_s([P, 2, P])
        wgT = sb("wgT", [P, 2, P])
        gate_diag = sb("gate_diag", [P, P])
        cols = sb("cols", [P, 16])
        C_BI, C_GATE, C_B1, C_B2, C_SUM = 0, 1, 2, 2 + RES, 2 + 2 * RES
        brow = sb("brow", [1, 2, 3, P])
        bpart = sb("bpart", [1, 2, 3, TPG, P], BF16)
        bias3 = sb("bias3", [3, 2, GW], BF16)
        row_buf = sb("row_buf", [P, EP])
        M_buf = sb("M_buf", [P, EP])
        G = sb("G", [P, EP])
        rows_nat = carve_s([P, 2, P], I32)
        w_rows = carve_s([P, P])
        rows_f = carve_s([P, 4, P])
        rows_i = carve_s([P, 2, P], I32)
        e_cols = carve_s([P, 5, ET])
        dst_idx = sb("dst_idx", [P, ET], I32)
        pos = sb("pos", [P, ET])
        pos_idx = sb("pos_idx", [P, ET], I32)
        meta = sb("meta", [P, ET, 4])
        src_s = sb("src_s", [P, ET + 1])
        w_s = sb("w_s", [P, ET])
        prev_last = sb("prev_last", [P, ET])
        same_next = sb("same_next", [P, ET])
        srcT = sb("srcT", [P, P])
        node_idx = sb("node_idx", [P, ET], I32)
        out_idx = sb("out_idx", [P, ET], I32)
        src_rows = row_buf[:].bitcast(I32)
        payload = M_buf[:, 0:ET * PW].rearrange("p (t w) -> p t w", w=PW)
        payload_i = M_buf[:, 0:ET * PW].bitcast(I32).rearrange("p (t w) -> p t w", w=PW)
        meta_i = meta[:].rearrange("p t w -> p (t w)").bitcast(I32).rearrange("p (t w) -> p t w", w=4)

        at = [0]

        def carve(words, dt=F32):
            v = G[:, at[0]:at[0] + words]
            at[0] += words
            return v if dt == F32 else v.bitcast(dt)

        oh_hi = [carve(DIG // 2, BF16) for _ in range(TPG)]
        oh_lo = [carve(DIG // 2, BF16) for _ in range(TPG)]
        hi_row = carve(GW, I32)
        oh_hiT = [carve(GW) for _ in range(2)]
        same = carve(P)
        junk = carve(DIG)
        acc_a, acc_b = carve(TPG), carve(TPG)
        cum = [carve(2 * DIG) for _ in range(2)]
        hist, incl, base, ptr_f = (carve(2 * DIG) for _ in range(4))
        zeros = carve(DIG)
        offs = carve(2)
        ptr_i = carve(2 * DIG, I32)

        seg_m = [sb(f"seg_m{h}", [P, 2 * P]) for h in range(2)]
        seg_T = [sb(f"seg_T{h}", [P, 2 * P]) for h in range(2)]

        at_m = [0]

        def carve_m(words):
            v = M_buf[:, at_m[0]:at_m[0] + words]
            at_m[0] += words
            return v

        X, X1, S, EL, H = ([carve_m(GW) for _ in range(CHAINS)] for _ in range(5))
        attr_in = [carve_m(TPG * R) for _ in range(CHAINS)]
        attrT = [H[c][:, 0:2 * P] for c in range(CHAINS)]
        zeros_w = carve_s([P, P])
        zeros_r = carve_s([P, GW])
        tick = sb("tick", [P, 1])
        seg_M = [carve_m(2 * P) for _ in range(2)]
        stats = [sb(f"stats{c}", [P, TPG, 6]) for c in range(CHAINS)]
        mv = [sb(f"mv{c}", [P, 2, TPG, 2]) for c in range(CHAINS)]
        ve = [sb(f"ve{c}", [P, 2, TPG]) for c in range(CHAINS)]
        rs = [sb(f"rs{c}", [P, 2, TPG]) for c in range(CHAINS)]
        nm = [sb(f"nm{c}", [P, TPG]) for c in range(CHAINS)]
        minus_half = sb("minus_half", [P, TPG])

        iotas, consts = sem("iotas"), sem("consts")
        w_loaded, b_loaded = sem("w_loaded"), sem("b_loaded")
        wT_psum, wT_ready = sem("wT_psum"), sem("wT_ready")
        bias_parts, bias_ready = sem("bias_parts"), sem("bias_ready")
        pads_set, rows_loaded, row_bcast = sem("pads_set"), sem("rows_loaded"), sem("row_bcast")
        pads_attr, attr_loaded = sem("pads_attr"), sem("attr_loaded")
        rows_split, cols_psum, cols_ready = sem("rows_split"), sem("cols_psum"), sem("cols_ready")
        idx_ready = sem("idx_ready")
        onehot_ready, hist_added = sem("onehot_ready"), sem("hist_added")
        scan_ready, offs_psum, ptr_ready, ptr_stored = sem("scan_ready"), sem("offs_psum"), sem("ptr_ready"), sem("ptr_stored")
        tile_onehots, onehotT_ready = sem("tile_onehots"), sem("onehotT_ready")
        cum_copied, cum_added, place_psum, place_read = sem("cum_copied"), sem("cum_added"), sem("place_psum"), sem("place_read")
        pos_ready, ptr_gathered, payload_set, scattered = sem("pos_ready"), sem("ptr_gathered"), sem("payload_set"), sem("scattered")
        meta_loaded, meta_split, near_psum, near_ready = sem("meta_loaded"), sem("meta_split"), sem("near_psum"), sem("near_ready")
        srcT_stored, srow_loaded, masks_ready = sem("srcT_stored"), sem("srow_loaded"), sem("masks_ready")
        zero_stored = sem("zero_stored")
        xd_gathered = sem("xd_gathered")
        tot_gathered = [sem(f"tot_gathered{k}") for k in range(3)]
        seg_in, seg_mm, seg_fixed, seg_tr, seg_rows = sem("seg_in"), sem("seg_mm"), sem("seg_fixed"), sem("seg_tr"), sem("seg_rows")
        seg_mask = sem("seg_mask")
        tot_stored = sem("tot_stored")
        srow_again, xs_gathered = sem("srow_again"), sem("xs_gathered")
        chain, link_sem, place_link = sem("carry_chain"), sem("link"), sem("place_link")
        srcT_ready, wg_zeroed = sem("srcT_ready"), sem("wg_zeroed")

        def chain_sems(pre):
            return {k: sem(f"{pre}_{k}") for k in
                    ("v", "stats", "mean", "var", "rstd", "x1", "xT", "exp_s", "s", "lin", "exp", "capped", "log", "sp",
                     "y", "nmean", "o", "u0", "attrT", "attr_copied", "g", "msg")}

        ms = chain_sems("msg")
        act_done, dve_done, pe_done, pool_done = ([sem(f"{e}_done{c}") for c in range(CHAINS)] for e in ("act", "dve", "pe", "pool"))
        edge_v, edge_u0 = sem("edge_v"), sem("edge_u0")
        attr_arrived = [sem(f"attr_arrived{c}") for c in range(CHAINS)]
        x_arrived = [sem(f"x_arrived{c}") for c in range(CHAINS)]
        out_stored = [sem(f"out_stored{c}") for c in range(CHAINS)]

        def runs_of(kinds):
            runs, before, used = [], 0, [0] * CHAINS
            for kind, count in kinds:
                for reps, n, first in plan(count):
                    runs.append((kind, reps, n, first, before, list(used)))
                    before += reps * n
                    for c in range(n):
                        used[c] += reps
            return runs, used

        msg_runs, _ = runs_of([("msg", EG)])

        GROUPS = NG + EG
        U, HB = 0, 4
        STEPS = [(U, C_BI, None)]
        for r in range(RES):
            STEPS.append((U, C_SUM + r - 1 if r else None, 3 + 2 * r))
            STEPS.append((HB, C_B1 + r, 4 + 2 * r))
        STEPS.append((U, C_SUM + RES - 1, 2))
        NSTEP = len(STEPS)
        LINS = NSTEP - 1
        SOFTPLUS = range(NSTEP)
        ACT_STEPS = ["exp s", "ln s"] + [(q, k) for k in SOFTPLUS for q in ("exp", "ln")] + ["norm"]
        DVE_STEPS = ["stats 1", "mean 1", "var 1", "x1"] + [(q, k) for k in SOFTPLUS for q in ("cap", "max")] + ["stats 2", "mean 2", "var 2", "nmean"]
        PE_STEPS = ["xT"] + [("lin", k) for k in range(LINS)] + ["y"]
        POOL_STEPS = ["rstd 1", "rstd 2"]

        def after(steps, use, step):
            return use * len(steps) + (steps.index(step) + 1)

        STEP_T, FIRST_T = 4, 7
        WINDOW = FIRST_T + STEP_T * NSTEP + 5
        assert WINDOW % CHAINS == 0 and (WINDOW // CHAINS) % 2 == 1

        def in_turn(ops):
            placed = []
            for when, op in ops:
                for c in range(CHAINS):
                    t = when + c * WINDOW // CHAINS
                    placed.append((t % WINDOW, c, int(t // WINDOW), op))
            return [(op, c, lag) for _, c, lag, op in sorted(placed, key=lambda q: q[:2])]

        LAST_W = (GROUPS - 1) // CHAINS + 1
        NODE_W, EDGE_W = NG // CHAINS, -(-NG // CHAINS) + 1
        WINDOWS = [0, 1, (2, NODE_W)] + list(range(NODE_W, EDGE_W + 1)) + [(EDGE_W + 1, GROUPS // CHAINS)] + list(range(GROUPS // CHAINS, LAST_W + 1))

        def each_window(eng, body, unrolled_from=None):
            for w in WINDOWS:
                if isinstance(w, int):
                    body(w, None)
                elif unrolled_from is not None and w[0] >= unrolled_from:
                    for one in range(*w):
                        body(one, None)
                else:
                    with eng.Fori(*w) as one:
                        body(one, "node" if w[1] <= NODE_W else "edge")

        def group_kind(w, c, lag, kind):
            if kind:
                return kind
            i = (w - lag) * CHAINS + c
            return None if i < 0 or i >= GROUPS else "node" if i < NG else "edge"

        def node_row(i):
            return min(i * GW, N - GW) if isinstance(i, int) else i * GW

        NODE_USES = [len(range(c, NG, CHAINS)) for c in range(CHAINS)]

        def each_run(eng, runs, body):
            for kind, reps, n, first, before, used in runs:
                if reps > 1:
                    with eng.Fori(0, reps) as g:
                        body(kind, n, g * n + first, g * n + before, [g + u for u in used])
                else:
                    body(kind, n, first, before, used)

        def nth(per, before, n, k, c):
            return before * per + (k * n + c + 1)

        def over_groups(eng, body, peel=True):
            if peel:
                body(0)
            with eng.Fori(int(peel), EG) as g:
                body(g)

        def later(value):
            return not (isinstance(value, int) and value == 0)

        block = ctx.enter_context(nc.Block())

        @block.sync
        def _(sp):
            for i, name in enumerate(order):
                sp.dma_start(w_nat[:, i, :], mats[name]).then_inc(w_loaded, 16)
            sp.wait_ge(wg_zeroed, 1)
            for i in range(2):
                sp.dma_start(wg_nat[:, i, i * R:(i + 1) * R], Wg).then_inc(w_loaded, 16)
            with nc.allow_non_contiguous_dma(reason="small columns"):
                for v, at_c in [(bi, C_BI), (gate, C_GATE)] + [(b1[k], C_B1 + k) for k in range(RES)] + [(b2[k], C_B2 + k) for k in range(RES)]:
                    sp.dma_start(cols[:, at_c:at_c + 1], v.rearrange("(p o) -> p o", o=1)).then_inc(b_loaded, 16)
            sp.dma_start(brow[:, 0, 0, :], bv.rearrange("(o f) -> o f", o=1)).then_inc(b_loaded, 16)
            sp.dma_start(brow[:, 1, 0, :], bj.rearrange("(o f) -> o f", o=1)).then_inc(b_loaded, 16)

            sp.wait_ge(pads_set, 5)
            for v, rows in ((src, rows_nat[:, 0, :]), (dst, rows_nat[:, 1, :]), (weight, w_rows[:])):
                sp.dma_start(rows[0:FULLT, :], v[0:FULLT * P].rearrange("(t p) -> t p", p=P)).then_inc(rows_loaded, 16)
                sp.dma_start(rows[FULLT:FULLT + 1, 0:TAIL], v[FULLT * P:E].rearrange("(o p) -> o p", o=1)).then_inc(rows_loaded, 16)
            sp.dma_start(src_rows[:, 0:E], src.rearrange("(o e) -> o e", o=1).to_broadcast([P, E])).then_inc(row_bcast, 16)
            sp.dma_start(payload[:, 0:FULLT, 4:PW], attr[0:FULLT * P].rearrange("(t p) f -> p t f", p=P)).then_inc(attr_loaded, 16)
            sp.dma_start(payload[0:TAIL, FULLT, 4:PW], attr[FULLT * P:E]).then_inc(attr_loaded, 16)
            sp.wait_ge(consts, 1)
            for k in range(3):
                sp.dma_start(totals[k][ZROW:ZROW + 1, :], zero_row[:]).then_inc(zero_stored, 16)
            sp.wait_ge(bias_parts, 1)
            for part in range(3):
                for q in range(2):
                    sp.dma_start(bias3[part:part + 1, q, :], bpart[:, q, part, :, :].rearrange("o a b -> o (a b)")).then_inc(bias_ready, 16)

            sp.wait_ge(ptr_ready, 1)
            sp.dma_start(ptr_table.rearrange("(c p l) o -> p c (l o)", c=2, l=DIG), ptr_i.rearrange("p (c l) -> p c l", c=2)).then_inc(ptr_stored, 16)

            sp.wait_ge(scattered, 16 * ET)
            with nc.allow_non_contiguous_dma(reason="four words of each row"):
                sp.dma_start(meta[:], sorted_rows.rearrange("(t p) w -> p t w", p=P)[:, :, 0:4]).then_inc(meta_loaded, 16)
            sp.wait_ge(srcT_ready, 1)
            sp.dma_start(sorted_src, srcT[0:ET, :]).then_inc(srcT_stored, 16)
            sp.wait_ge(srcT_stored, 16)
            sp.dma_start(row_buf[:], sorted_src.rearrange("t p -> (t p)").rearrange("(o e) -> o e", o=1).to_broadcast([P, EP])).then_inc(srow_loaded, 16)

            for k in range(3):
                with sp.Fori(0, EG) as g:
                    sp.wait_ge(seg_rows, (g + EG * k) * 2 + 2)
                    sp.dma_start(totals[k][bass.ds(g * GW, GW), :].rearrange("(j p) f -> p j f", p=P),
                                 G[:, bass.ds(g * GW, GW)].rearrange("p (j f) -> p j f", f=F)).then_inc(tot_stored, 16)

            def attr_loads(kind, n, grp, before, used):
                if later(before):
                    sp.wait_ge(ms["attrT"], before)
                for c in range(n):
                    sp.dma_start(attr_in[c].rearrange("p (j r) -> p j r", r=R),
                                 sorted_rows[bass.ds((grp + c) * GW, GW), :].rearrange("(j p) w -> p j w", p=P)[:, :, 4:PW]).then_inc(attr_arrived[c], 16)

            sp.wait_ge(seg_mm, 2 * EG * 3)
            each_run(sp, msg_runs, attr_loads)

            sp.wait_ge(ms["v"], EG)
            sp.dma_start(row_buf[:], sorted_src.rearrange("t p -> (t p)").rearrange("(o e) -> o e", o=1).to_broadcast([P, EP])).then_inc(srow_again, 16)

            def node_loads(w, kind):
                for c in range(CHAINS):
                    of = group_kind(w, c, 0, kind)
                    if of is None:
                        continue
                    if later(w):
                        sp.wait_ge(dve_done[c], after(DVE_STEPS, w - 1, "x1"))
                    i = w * CHAINS + c
                    Xc = X[c].rearrange("p (j f) -> p j f", f=F)
                    if of == "node":
                        sp.dma_start(Xc, x[bass.ds(node_row(i), GW), :].rearrange("(p j) f -> p j f", j=TPG)).then_inc(x_arrived[c], 16)
                    else:
                        sp.dma_start(Xc, totals[2][bass.ds((i - NG) * GW, GW), :].rearrange("(j p) f -> p j f", p=P)).then_inc(x_arrived[c], 16)

            sp.wait_ge(ms["x1"], EG)
            each_window(sp, node_loads)

        @block.gpsimd
        def _(pool):
            exact = dict(allow_small_or_imprecise_dtypes=True)
            pool.iota(col_minus_row[:], [[1, P]], base=0, channel_multiplier=-1, **exact).then_inc(iotas, 1)
            pool.iota(row_no[:], [[0, P]], base=0, channel_multiplier=1, **exact).then_inc(iotas, 1)
            pool.iota(digits[:], [[1, DIG]], base=0, channel_multiplier=0, **exact).then_inc(iotas, 1)
            pool.iota(hi_no[:], [[P, 2]], base=0, channel_multiplier=1, **exact).then_inc(iotas, 1)
            pool.iota(rows_nat[:, 0, :], [[1, P]], base=N - E, channel_multiplier=P).then_inc(pads_set, 1)
            pool.memset(rows_nat[:, 1, :], 0).then_inc(pads_set, 1)
            pool.memset(w_rows[:], 0.0).then_inc(pads_set, 1)
            pool.iota(src_rows[:, E:EP], [[1, EP - E]], base=N, channel_multiplier=0).then_inc(pads_set, 1)
            pool.memset(payload[:, FULLT:ET, :], 0.0).then_inc(pads_set, 1)
            pool.memset(minus_half[:], -0.5).then_inc(iotas, 1)

            pool.wait_ge(ptr_stored, 16)
            pool.wait_ge(idx_ready, 1)
            pool.wait_ge(attr_loaded, 32)
            for t in range(ET):
                pool.indirect_dma_start(payload_i[:, t, 2:3], None, ptr_table,
                                        bass.IndirectOffsetOnAxis(ap=dst_idx[:, t:t + 1], axis=0)).then_inc(ptr_gathered, 16)
            pool.wait_ge(ptr_gathered, 16 * ET)
            pool.wait_ge(pos_ready, 1)
            pool.wait_ge(payload_set, 1)
            for t in range(ET):
                pool.indirect_dma_start(sorted_rows, bass.IndirectOffsetOnAxis(ap=pos_idx[:, t:t + 1], axis=0),
                                        payload[:, t, :], None).then_inc(scattered, 16)
            pool.wait_ge(masks_ready, EG)
            for t in range(ET):
                pool.indirect_dma_start(row_buf[:, t * P:(t + 1) * P], None, x,
                                        bass.IndirectOffsetOnAxis(ap=meta_i[:, t, 1:2], axis=0)).then_inc(xd_gathered, 16)
            pool.wait_ge(zero_stored, 48)
            for k in range(3):
                pool.wait_ge(tot_stored, 16 * EG * (k + 1))
                for t in range(ET):
                    pool.indirect_dma_start(G[:, t * P:(t + 1) * P], None, totals[k],
                                            bass.IndirectOffsetOnAxis(ap=meta_i[:, t, 2:3], axis=0)).then_inc(tot_gathered[k], 16)

            def rstd(sems, per, n, before, k):
                for c in range(n):
                    pool.wait_ge(sems["var"], nth(per, before, n, k, c))
                    pool.tensor_tensor(rs[c][:, k, :], ve[c][:, k, :], minus_half[:], ALU.pow).then_inc(sems["rstd"], 1)

            each_run(pool, msg_runs, lambda kind, n, grp, before, used: rstd(ms, 1, n, before, 0))

            pool.wait_ge(seg_in, 2 * EG * 4)
            for t in range(ET):
                pool.indirect_dma_start(row_buf[:, t * P:(t + 1) * P], None, x,
                                        bass.IndirectOffsetOnAxis(ap=node_idx[:, t:t + 1], axis=0)).then_inc(xs_gathered, 16)

            POOL_OPS = in_turn([(1.0, "rstd 1"), (40.8, "rstd 2"), (44.5, "store")])

            def pool_window(w, kind):
                for op, c, lag in POOL_OPS:
                    of, use = group_kind(w, c, lag, kind), w - lag
                    if of is None:
                        continue
                    if op == "rstd 1":
                        pool.wait_ge(dve_done[c], after(DVE_STEPS, use, "var 1"))
                        pool.tensor_tensor(rs[c][:, 0, :], ve[c][:, 0, :], minus_half[:], ALU.pow).then_inc(pool_done[c], 1)
                    elif op == "rstd 2":
                        pool.wait_ge(dve_done[c], after(DVE_STEPS, use, "var 2"))
                        pool.tensor_tensor(rs[c][:, 1, :], ve[c][:, 1, :], minus_half[:], ALU.pow).then_inc(pool_done[c], 1)
                    elif of == "node":
                        pool.wait_ge(act_done[c], after(ACT_STEPS, use, "norm"))
                        i = use * CHAINS + c
                        if isinstance(i, int) and i == NG - 1:
                            pool.wait_ge(out_stored[(i - 1) % CHAINS], 16 * ((i - 1) // CHAINS + 1))
                        pool.dma_start(out[bass.ds(node_row(i), GW), :].rearrange("(p j) f -> p j f", j=TPG),
                                       H[c].rearrange("p (j f) -> p j f", f=F)).then_inc(out_stored[c], 16)
                    else:
                        i = use * CHAINS + c - NG
                        if i == 0:
                            for other in range(CHAINS):
                                pool.wait_ge(out_stored[other], 16 * NODE_USES[other])
                        pool.wait_ge(act_done[c], after(ACT_STEPS, use, "norm"))
                        for j in range(TPG):
                            pool.indirect_dma_start(out, bass.IndirectOffsetOnAxis(ap=out_idx[:, i * TPG + j:i * TPG + j + 1], axis=0),
                                                    H[c][:, j * P:(j + 1) * P], None,
                                                    bounds_check=N - 1, oob_is_err=False).then_inc(out_stored[c], 16)

            each_window(pool, pool_window, unrolled_from=EDGE_W)
            for c in range(CHAINS):
                edge_uses = len(range(c, GROUPS, CHAINS)) - NODE_USES[c]
                pool.wait_ge(out_stored[c], 16 * NODE_USES[c] + 16 * TPG * edge_uses)

        def act_source(sems, n, before):
            act = nc.scalar
            for c in range(n):
                act.wait_ge(sems["xT"], nth(1, before, n, 0, c))
                act.activation(EL[c], bank[:, 4 + c, :], ACT.Exp).then_inc(sems["exp_s"], 1)
            for c in range(n):
                act.wait_ge(sems["exp_s"], nth(1, before, n, 0, c))
                act.activation(S[c], EL[c], ACT.Ln, bias=1.0).then_inc(sems["s"], 1)

        def act_softplus(sems, per, k, n, before, ready, bank0, bias):
            act = nc.scalar
            for c in range(n):
                ready(act, c)
                if bias is None:
                    act.activation(EL[c], bank[:, bank0 + c, :], ACT.Exp).then_inc(sems["exp"], 1)
                else:
                    act.activation(EL[c], bank[:, bank0 + c, :], ACT.Exp, bias=cols[:, bias:bias + 1]).then_inc(sems["exp"], 1)
            for c in range(n):
                act.wait_ge(sems["capped"], nth(per, before, n, k, c))
                act.activation(EL[c], EL[c], ACT.Ln, bias=1.0).then_inc(sems["log"], 1)

        def act_msg(kind, n, grp, before, used):
            act = nc.scalar
            for c in range(n):
                act.wait_ge(ms["attrT"], nth(1, before, n, 0, c))
                act.copy(attrT[c], bank[:, c, 0:2 * P]).then_inc(ms["attr_copied"], 1)
            act_source(ms, n, before)
            act_softplus(ms, 1, 0, n, before, lambda e, c: e.wait_ge(ms["lin"], nth(1, before, n, 0, c)), 4, None)

        ACT_OPS = in_turn([(4, "exp s"), (5, "ln s"), (43, "norm")]
                          + [(FIRST_T + STEP_T * k, ("exp", k)) for k in range(NSTEP)]
                          + [(FIRST_T + STEP_T * k + 1.1, ("ln", k)) for k in range(NSTEP)])

        def act_window(w, kind):
            act = nc.scalar
            for op, c, lag in ACT_OPS:
                of, use = group_kind(w, c, lag, kind), w - lag
                if of is None:
                    continue
                if op == "exp s":
                    act.wait_ge(pe_done[c], after(PE_STEPS, use, "xT"))
                    act.activation(EL[c], bank[:, HB + c, :], ACT.Exp).then_inc(act_done[c], 1)
                elif op == "ln s":
                    act.wait_ge(act_done[c], after(ACT_STEPS, use, "exp s"))
                    act.activation(S[c], EL[c], ACT.Ln, bias=1.0).then_inc(act_done[c], 1)
                elif op == "norm":
                    act.wait_ge(dve_done[c], after(DVE_STEPS, use, "nmean"))
                    for j in range(TPG):
                        cw = slice(j * P, (j + 1) * P)
                        last = act.activation(H[c][:, cw], bank[:, HB + c, cw], ACT.Identity, bias=nm[c][:, j:j + 1], scale=rs[c][:, 1, j:j + 1])
                    last.then_inc(act_done[c], 1)
                elif op[0] == "exp":
                    k = op[1]
                    bank0, bias, _ = STEPS[k]
                    if k == 1:
                        act.wait_ge(dve_done[c], after(DVE_STEPS, use, ("max", 0)))
                    else:
                        act.wait_ge(pe_done[c], after(PE_STEPS, use, ("lin", max(k - 1, 0))))
                    if bias is None:
                        act.activation(EL[c], bank[:, bank0 + c, :], ACT.Exp).then_inc(act_done[c], 1)
                    else:
                        act.activation(EL[c], bank[:, bank0 + c, :], ACT.Exp, bias=cols[:, bias:bias + 1]).then_inc(act_done[c], 1)
                else:
                    act.wait_ge(dve_done[c], after(DVE_STEPS, use, ("cap", op[1])))
                    act.activation(EL[c], EL[c], ACT.Ln, bias=1.0).then_inc(act_done[c], 1)

        @block.scalar
        def _(act):
            act.preload_act_table_set("natural_log_exp_and_others")
            act.wait_ge(wT_psum, 1)
            act.copy(wT[:, 0:TPG, :], bank[:, 0, :].rearrange("p (j f) -> p j f", f=P)).then_inc(wT_ready, 1)
            act.copy(wT[:, TPG:2 * TPG, :], bank[:, 1, :].rearrange("p (j f) -> p j f", f=P)).then_inc(wT_ready, 1)
            act.copy(wT[:, 2 * TPG, :], bank[:, 2, 0:P]).then_inc(wT_ready, 1)
            act.copy(wgT[:], bank[:, 3, 0:2 * P].rearrange("p (i f) -> p i f", f=P)).then_inc(wT_ready, 1)

            def copy_counts(g):
                for j in range(TPG):
                    act.wait_ge(cum_added, g * TPG + j + 1)
                    if later(g) or j > 1:
                        act.wait_ge(place_psum, g * TPG + j - 1)
                    act.copy(cum[j % 2], bank[:, 0, :]).then_inc(cum_copied, 1)

            over_groups(act, copy_counts)

            for k in range(4):
                with act.Fori(0, EG) as g:
                    done = (g + EG * k) * 2
                    for h in range(2):
                        cols_of = bass.ds(g * GW + h * 2 * P, 2 * P)
                        if k < 3:
                            act.wait_ge(seg_tr, done + h + 1)
                            act.copy(G[:, cols_of], bank[:, 2 + h, 0:2 * P]).then_inc(seg_rows, 1)
                        else:
                            act.wait_ge(seg_fixed, done + h + 1)
                            act.copy(G[:, cols_of], seg_T[h][:]).then_inc(seg_rows, 1)
                if k == 2:
                    each_run(act, msg_runs, act_msg)

            each_window(act, act_window)

        @block.tensor
        def _(pe):
            pe.wait_ge(consts, 1)
            pe.wait_ge(w_loaded, 16 * (len(order) + 2))
            for i in range(len(order)):
                pe.transpose(bank[:, i // TPG, (i % TPG) * P:(i % TPG + 1) * P], w_nat[:, i, :], ident[:])
            for i in range(2):
                mm = pe.transpose(bank[:, 3, i * P:(i + 1) * P], wg_nat[:, i, :], ident[:])
            mm.then_inc(wT_psum, 1)

            pe.wait_ge(rows_split, 1)
            pe.wait_ge(wT_ready, 4)
            for q in range(4):
                pe.transpose(bank[:, 4, q * P:(q + 1) * P], rows_f[:, q, :], ident[:])
            pe.transpose(bank[:, 5, 0:P], w_rows[:], ident[:]).then_inc(cols_psum, 1)

            pe.matmul(bank[:, 0, :], zeros_w[:], zeros_r[:], start=True, stop=False, skip_group_check=True)
            with pe.Fori(0, EG) as g:
                for j in range(TPG):
                    pe.wait_ge(onehot_ready, g * TPG + j + 1)
                    for c in range(2):
                        mm = pe.matmul(bank[:, 0, c * DIG:(c + 1) * DIG], oh_hi[j][:, c * P:(c + 1) * P], oh_lo[j],
                                       start=False, stop=True, skip_group_check=True)
                    mm.then_inc(hist_added, 1)
            pe.wait_ge(scan_ready, 1)
            pe.matmul(bank[:, 1, 0:1], below[:], incl[:, DIG - 1:DIG], start=True, stop=True)
            pe.matmul(bank[:, 1, 1:2], below[:], incl[:, 2 * DIG - 1:2 * DIG], start=True, stop=False)
            pe.matmul(bank[:, 1, 1:2], ones[:], incl[:, DIG - 1:DIG], start=False, stop=True).then_inc(offs_psum, 1)

            pe.wait_ge(ptr_ready, 1)
            pe.matmul(bank[:, 0, :], ident[:], base, start=True, stop=False, skip_group_check=True).then_inc(cum_added, 1)
            def place_products(g):
                pe.wait_ge(onehotT_ready, g + 1)
                for j in range(TPG):
                    pe.wait_ge(cum_copied, g * TPG + j + 1)
                    pe.wait_ge(tile_onehots, g * TPG + j + 1)
                    for c in range(2):
                        mm = pe.matmul(bank[:, 0, c * DIG:(c + 1) * DIG], oh_hi[j][:, c * P:(c + 1) * P], oh_lo[j],
                                       start=False, stop=True, skip_group_check=True)
                    mm.then_inc(cum_added, 1)
                    if later(g) or j > 1:
                        pe.wait_ge(place_read, g * TPG + j - 1)
                    for c in range(2):
                        mm = pe.matmul(bank[:, 2 + j % 2, 0:DIG], oh_hiT[c][:, j * P:(j + 1) * P], cum[j % 2][:, c * DIG:(c + 1) * DIG],
                                       start=(c == 0), stop=(c == 1))
                    mm.then_inc(place_psum, 1)

            over_groups(pe, place_products)

            pe.wait_ge(meta_split, 1)
            pe.matmul(bank[:, 4, 0:ET], pick_last[:], src_s[:, 0:ET], start=True, stop=True)
            pe.matmul(bank[:, 4, P:P + ET], shift_up[:], src_s[:, 0:ET], start=True, stop=False, skip_group_check=True)
            pe.matmul(bank[:, 4, P:P + ET], wrap[:], src_s[:, 1:ET + 1], start=False, stop=True, skip_group_check=True)
            pe.transpose(bank[0:ET, 5, 0:P], src_s[:, 0:ET], ident[:]).then_inc(near_psum, 1)

            def segment_products(k):
                def products(g):
                    done = (g + EG * k) * 2
                    if later(done):
                        pe.wait_ge(seg_fixed, done)
                    for h in range(2):
                        pe.wait_ge(seg_in, done + h + 1)
                        for j in range(2):
                            w = slice(j * P, (j + 1) * P)
                            masks = M_buf[:, bass.ds(g * GW + (2 * h + j) * P, P)] if k < 3 else seg_M[h][:, w]
                            mm = pe.matmul(bank[:, h, w], seg_m[h][:, w], masks, start=True, stop=True)
                        mm.then_inc(seg_mm, 1)
                    if k < 3:
                        for h in range(2):
                            pe.wait_ge(seg_fixed, done + h + 1)
                            if later(done):
                                pe.wait_ge(seg_rows, done)
                            for j in range(2):
                                w = slice(j * P, (j + 1) * P)
                                mm = pe.transpose(bank[:, 2 + h, w], seg_T[h][:, w], ident[:])
                            mm.then_inc(seg_tr, 1)

                over_groups(pe, products, peel=(k == 0))

            def transposes(sems, n, before):
                for c in range(n):
                    pe.wait_ge(sems["x1"], nth(1, before, n, 0, c))
                    for j in range(TPG):
                        w = slice(j * P, (j + 1) * P)
                        mm = pe.transpose(bank[:, HB + c, w], X1[c][:, w], ident[:])
                    mm.then_inc(sems["xT"], 1)

            def pe_msg(kind, n, grp, before, used):
                for c in range(n):
                    pe.wait_ge(attr_arrived[c], (used[c] + 1) * 16)
                    if later(before):
                        pe.wait_ge(ms["msg"], before)
                    for i in range(2):
                        mm = pe.transpose(bank[:, U + c, i * P:(i + 1) * P], attr_in[c][:, i * P:(i + 1) * P], ident[:])
                    mm.then_inc(ms["attrT"], 1)
                transposes(ms, n, before)
                for c in range(n):
                    pe.wait_ge(ms["attr_copied"], nth(1, before, n, 0, c))
                    for j in range(TPG):
                        w = slice(j * P, (j + 1) * P)
                        mm = pe.matmul(bank[:, U + c, w], attrT[c][:, (j // 2) * P:(j // 2 + 1) * P], wgT[:, j % 2, :], start=True, stop=True)
                    mm.then_inc(ms["g"], 1)
                for c in range(n):
                    pe.wait_ge(ms["s"], nth(1, before, n, 0, c))
                    pe.matmul(bank[:, HB + c, :], ones_bf[0:3, :], bias3[:, 1, :], start=True, stop=False, skip_group_check=True)
                    for j in range(TPG):
                        w = slice(j * P, (j + 1) * P)
                        mm = pe.matmul(bank[:, HB + c, w], S[c][:, w], wT[:, 1, :], start=False, stop=True, skip_group_check=True)
                    mm.then_inc(ms["lin"], 1)

            PE_OPS = in_turn([(3, "xT"), (6, "lin 0"), (FIRST_T + STEP_T * (NSTEP - 1) + 2.6, "y")]
                             + [(FIRST_T + STEP_T * k + 2.6, k) for k in range(1, NSTEP - 1)])

            def pe_window(w, kind):
                for op, c, lag in PE_OPS:
                    of, use = group_kind(w, c, lag, kind), w - lag
                    if of is None:
                        continue
                    if op == "xT":
                        pe.wait_ge(dve_done[c], after(DVE_STEPS, use, "x1"))
                        if later(use):
                            pe.wait_ge(act_done[c], after(ACT_STEPS, use - 1, "norm"))
                        for j in range(TPG):
                            cw = slice(j * P, (j + 1) * P)
                            mm = pe.transpose(bank[:, HB + c, cw], X1[c][:, cw], ident[:])
                        mm.then_inc(pe_done[c], 1)
                    elif op == "lin 0":
                        pe.wait_ge(act_done[c], after(ACT_STEPS, use, "ln s"))
                        pe.matmul(bank[:, U + c, :], wT[:, 0, :], S[c], start=True, stop=True, skip_group_check=True).then_inc(pe_done[c], 1)
                    elif op == "y":
                        pe.wait_ge(dve_done[c], after(DVE_STEPS, use, ("max", NSTEP - 1)))
                        pe.matmul(bank[:, HB + c, :], ones_bf[0:3, :], bias3[:, 0, :], start=True, stop=False, skip_group_check=True)
                        pe.matmul(bank[:, HB + c, :], ident[:], X1[c], start=False, stop=False, skip_group_check=True)
                        for j in range(TPG):
                            cw = slice(j * P, (j + 1) * P)
                            pe.matmul(bank[:, HB + c, cw], S[c][:, cw], gate_diag[:], start=False, stop=False, skip_group_check=True)
                            mm = pe.matmul(bank[:, HB + c, cw], H[c][:, cw], wT[:, 2, :], start=False, stop=True, skip_group_check=True)
                        mm.then_inc(pe_done[c], 1)
                    else:
                        bank0, _, w_at = STEPS[op]
                        pe.wait_ge(dve_done[c], after(DVE_STEPS, use, ("max", op)))
                        pe.matmul(bank[:, (HB if bank0 == U else U) + c, :], wT[:, w_at, :], H[c],
                                  start=(bank0 == U), stop=True, skip_group_check=True).then_inc(pe_done[c], 1)

            for k in range(3):
                segment_products(k)
            pe.wait_ge(bias_ready, 96)
            pe.wait_ge(seg_rows, 2 * EG * 3)
            each_run(pe, msg_runs, pe_msg)
            pe.wait_ge(ms["msg"], EG)
            segment_products(3)
            pe.wait_ge(seg_fixed, 2 * EG * 4)
            each_window(pe, pe_window)

        @block.vector
        def _(dve):
            links = [0]

            def link(ins):
                links[0] += 1
                ins.then_inc(link_sem, 1)
                dve.wait_ge(link_sem, links[0])

            dve.memset(wg_nat, 0.0).then_inc(wg_zeroed, 1)
            dve.memset(zero_row[:], 0.0)
            dve.memset(ones[:], 1.0)
            dve.memset(ones_bf[:], 1.0)
            dve.memset(zeros_w[:], 0.0)
            dve.memset(zeros_r[:], 0.0)
            dve.memset(seg_T[0][:], 0.0)
            dve.memset(seg_T[1][:], 0.0)
            dve.memset(src_s[:, ET:ET + 1], -1.0)
            dve.memset(prev_last[:, 0:1], -1.0)
            dve.wait_ge(iotas, 5)
            dve.tensor_scalar(ident[:], col_minus_row[:], 0.0, None, ALU.is_equal)
            dve.tensor_scalar(below[:], col_minus_row[:], 0.0, None, ALU.is_gt)
            dve.tensor_scalar(earlier[:], col_minus_row[:], 0.0, None, ALU.is_lt)
            dve.tensor_scalar(shift_up[:], col_minus_row[:], -1.0, None, ALU.is_equal)
            dve.tensor_scalar(pick_last[:], row_no[:], float(P - 1), None, ALU.is_equal)
            link(dve.tensor_scalar(wrap[:], col_minus_row[:], float(P - 1), None, ALU.is_equal))
            dve.wait_ge(b_loaded, 16 * (4 + 2 * RES))
            link(dve.tensor_scalar(gate_diag[:], ident[:], cols[:, C_GATE:C_GATE + 1], None, ALU.mult))
            link(dve.tensor_copy(cols[:, C_SUM:C_SUM + 1], cols[:, C_B2:C_B2 + 1]))
            for k in range(1, RES):
                link(dve.tensor_tensor(cols[:, C_SUM + k:C_SUM + k + 1], cols[:, C_SUM + k - 1:C_SUM + k], cols[:, C_B2 + k:C_B2 + k + 1], ALU.add))
            dve.memset(tick[:], 0.0).then_inc(consts, 1)
            for part in range(3):
                link(dve.tensor_copy(bpart[:, :, part, 0, :], brow[:, :, part, :]))
                if part < 2:
                    link(dve.tensor_tensor(brow[:, :, part + 1, :], brow[:, :, part, :], bpart[:, :, part, 0, :], ALU.subtract))
                for r in range(1, TPG):
                    last = dve.tensor_copy(bpart[:, :, part, r, :], bpart[:, :, part, 0, :])
            last.then_inc(bias_parts, 1)

            dve.wait_ge(rows_loaded, 96)
            dve.tensor_copy(rows_f[:, 0, :], rows_nat[:, 0, :])
            dve.tensor_copy(rows_f[:, 3, :], rows_nat[:, 1, :])
            dve.tensor_scalar(rows_i[:, 0, :], rows_nat[:, 0, :], 8, None, ALU.logical_shift_right)
            link(dve.tensor_scalar(rows_i[:, 1, :], rows_nat[:, 0, :], DIG - 1, None, ALU.bitwise_and))
            dve.tensor_copy(rows_f[:, 1:3, :], rows_i[:, :, :]).then_inc(rows_split, 1)
            dve.wait_ge(cols_psum, 1)
            dve.tensor_copy(e_cols[:, 0:4, :], bank[:, 4, :].rearrange("p (q t) -> p q t", q=4)[:, :, 0:ET])
            link(dve.tensor_copy(e_cols[:, 4, :], bank[:, 5, 0:ET]))
            dve.tensor_copy(dst_idx[:], e_cols[:, 3, :]).then_inc(idx_ready, 1)
            dve.wait_ge(attr_loaded, 32)
            dve.wait_ge(idx_ready, 1)
            dve.tensor_copy(payload[:, :, 0], e_cols[:, 0, :])
            dve.tensor_copy(payload_i[:, :, 1], dst_idx[:])
            dve.tensor_copy(payload[:, :, 3], e_cols[:, 4, :]).then_inc(payload_set, 1)

            def count_onehots(g):
                if later(g):
                    dve.wait_ge(hist_added, g * TPG)
                for j in range(TPG):
                    t = bass.ds(g * TPG + j, 1)
                    dve.tensor_scalar(oh_hi[j], digits[:], e_cols[:, 1, t], None, ALU.is_equal)
                    dve.tensor_scalar(oh_lo[j], digits[:], e_cols[:, 2, t], None, ALU.is_equal).then_inc(onehot_ready, 1)

            over_groups(dve, count_onehots)
            dve.memset(zeros, 0.0)
            dve.wait_ge(hist_added, ET)
            link(dve.tensor_copy(hist, bank[:, 0, :]))
            for c in range(2):
                w = slice(c * DIG, (c + 1) * DIG)
                last = dve.tensor_tensor_scan(incl[:, w], hist[:, w], zeros, 0.0, ALU.add, ALU.add)
            last.then_inc(scan_ready, 1)
            dve.wait_ge(offs_psum, 1)
            link(dve.tensor_copy(offs, bank[:, 1, 0:2]))
            for c in range(2):
                w = slice(c * DIG, (c + 1) * DIG)
                dve.scalar_tensor_tensor(out=base[:, w], in0=incl[:, w], scalar=offs[:, c:c + 1], in1=hist[:, w], op0=ALU.add, op1=ALU.subtract)
                link(dve.tensor_scalar(ptr_f[:, w], incl[:, w], offs[:, c:c + 1], float(-1 - ZROW), ALU.add, ALU.add))
            link(dve.tensor_scalar(hist, hist, 1.0, None, ALU.min))
            link(dve.tensor_tensor(ptr_f, ptr_f, hist, ALU.mult))
            dve.tensor_scalar(ptr_i, ptr_f, float(ZROW), None, ALU.add).then_inc(ptr_ready, 1)

            dve.wait_ge(row_bcast, 16)
            def places(g):
                chunk = bass.ds(g * GW, GW)
                if later(g):
                    dve.wait_ge(place_psum, g * TPG)
                dve.tensor_scalar(hi_row, src_rows[:, chunk], 8, None, ALU.logical_shift_right).then_inc(place_link, 1)
                dve.wait_ge(place_link, g * (2 + 2 * TPG) + 1)
                dve.tensor_scalar(oh_hiT[0], hi_row, hi_no[:, 0:1], None, ALU.is_equal)
                dve.tensor_scalar(oh_hiT[1], hi_row, hi_no[:, 1:2], None, ALU.is_equal).then_inc(onehotT_ready, 1)
                for j in range(TPG):
                    t = bass.ds(g * TPG + j, 1)
                    dve.tensor_scalar(oh_hi[j], digits[:], e_cols[:, 1, t], None, ALU.is_equal)
                    dve.tensor_scalar(oh_lo[j], digits[:], e_cols[:, 2, t], None, ALU.is_equal).then_inc(tile_onehots, 1)
                for j in range(TPG):
                    t = bass.ds(g * TPG + j, 1)
                    dve.tensor_scalar(same, src_rows[:, bass.ds(g * GW + j * P, P)], e_cols[:, 0, t], None, ALU.is_equal).then_inc(place_link, 1)
                    dve.wait_ge(place_link, g * (2 + 2 * TPG) + 2 + 2 * j)
                    dve.tensor_tensor_reduce(junk[:, 0:P], same, earlier[:], 1.0, 0.0, ALU.mult, ALU.add, acc_b[:, j:j + 1]).then_inc(place_link, 1)
                    dve.wait_ge(place_link, g * (2 + 2 * TPG) + 3 + 2 * j)
                    dve.wait_ge(place_psum, g * TPG + j + 1)
                    last = dve.tensor_tensor_reduce(junk, bank[:, 2 + j % 2, 0:DIG], oh_lo[j], 1.0, 0.0, ALU.mult, ALU.add, acc_a[:, j:j + 1])
                    last.then_inc(place_read, 1)
                dve.wait_ge(place_read, g * TPG + TPG)
                dve.tensor_tensor(pos[:, bass.ds(g * TPG, TPG)], acc_a, acc_b, ALU.add).then_inc(place_link, 1)
                dve.wait_ge(place_link, g * (2 + 2 * TPG) + 2 + 2 * TPG)

            over_groups(dve, places)
            dve.tensor_copy(pos_idx[:], pos[:]).then_inc(pos_ready, 1)

            dve.wait_ge(meta_loaded, 16)
            dve.tensor_copy(w_s[:], meta[:, :, 3])
            dve.tensor_copy(src_s[:, 0:ET], meta[:, :, 0]).then_inc(meta_split, 1)
            dve.wait_ge(near_psum, 1)
            dve.tensor_copy(srcT[0:ET, :], bank[0:ET, 5, 0:P]).then_inc(srcT_ready, 1)
            dve.tensor_copy(prev_last[:, 1:ET], bank[:, 4, 0:ET - 1])
            link(dve.tensor_tensor(same_next[:], src_s[:, 0:ET], bank[:, 4, P:P + ET], ALU.is_equal))
            link(dve.scalar_tensor_tensor(out=pos[:], in0=same_next[:], scalar=FAR, in1=src_s[:, 0:ET], op0=ALU.mult, op1=ALU.add))
            dve.tensor_copy(out_idx[:], pos[:])
            link(dve.tensor_scalar(same_next[:], src_s[:, 0:ET], float(N - 1), None, ALU.min))
            link(dve.tensor_copy(node_idx[:], same_next[:]))
            dve.wait_ge(srow_loaded, 16)
            with dve.Fori(0, EG) as g:
                for j in range(TPG):
                    t = bass.ds(g * TPG + j, 1)
                    tile = bass.ds(g * GW + j * P, P)
                    dve.tensor_scalar(M_buf[:, tile], row_buf[:, tile], src_s[:, t], w_s[:, t], ALU.is_equal, ALU.mult)
                    last = dve.tensor_scalar(carry_mask[:, tile], row_buf[:, tile], prev_last[:, t], None, ALU.is_equal)
                last.then_inc(masks_ready, 1)
            dve.wait_ge(masks_ready, EG)

            def segment_sums(k):
                if k == 0:
                    dve.wait_ge(xd_gathered, 16 * ET)
                elif k < 3:
                    dve.wait_ge(tot_gathered[k - 1], 16 * ET)
                else:
                    dve.wait_ge(srow_again, 16)
                def sums(g):
                    done = (g + EG * k) * 2
                    for h in range(2):
                        half = bass.ds(g * GW + 2 * h * P, 2 * P)
                        if k == 0:
                            ins = dve.tensor_copy(seg_m[h][:], row_buf[:, half])
                        elif k < 3:
                            ins = dve.tensor_tensor(seg_m[h][:], row_buf[:, half], G[:, half], ALU.add)
                        else:
                            dve.tensor_copy(seg_m[h][:], G[:, half])
                            for j in range(2):
                                ins = dve.tensor_scalar(seg_M[h][:, j * P:(j + 1) * P], row_buf[:, bass.ds(g * GW + (2 * h + j) * P, P)],
                                                        src_s[:, bass.ds(g * TPG + 2 * h + j, 1)], None, ALU.is_equal)
                        ins.then_inc(seg_in, 1)
                    if later(done):
                        dve.wait_ge(seg_rows, done)
                    for h in range(2):
                        dve.wait_ge(seg_mm, done + h + 1)
                        for j in range(2):
                            i = 2 * h + j
                            before_T = seg_T[1 - h] if j == 0 else seg_T[h]
                            carry = before_T[:, 2 * P - 1:2 * P] if j == 0 else before_T[:, P - 1:P]
                            if later(done) or i:
                                dve.wait_ge(chain, (g + EG * k) * TPG + i)
                            w = slice(j * P, (j + 1) * P)
                            ins = dve.scalar_tensor_tensor(out=seg_T[h][:, w], in0=carry_mask[:, bass.ds(g * GW + i * P, P)], scalar=carry,
                                                           in1=bank[:, h, w], op0=ALU.mult, op1=ALU.add)
                            ins.then_inc(chain, 1)
                        dve.wait_ge(chain, (g + EG * k) * TPG + 2 * h + 2)
                        dve.memset(tick[:], 0.0).then_inc(seg_fixed, 1)

                over_groups(dve, sums, peel=(k == 0))

            def ln_stats(sems, per, k, n, before, src_of, ready):
                for c in range(n):
                    ready(c)
                    for j in range(TPG):
                        last = dve.bn_stats(stats[c][:, j, :], src_of[c][:, j * P:(j + 1) * P])
                    last.then_inc(sems["stats"], 1)
                dve.wait_ge(sems["stats"], nth(per, before, n, k, n - 1))
                dve.memset(tick[:], 0.0)
                for c in range(n):
                    for j in range(TPG):
                        last = dve.bn_aggr(mv[c][:, k, j, :], stats[c][:, j, :])
                    last.then_inc(sems["mean"], 1)
                for c in range(n):
                    dve.wait_ge(sems["mean"], nth(per, before, n, k, c))
                    dve.tensor_scalar(ve[c][:, k, :], mv[c][:, k, :, 1], EPS / 4 if k == 0 else EPS, None, ALU.add).then_inc(sems["var"], 1)

            def normalise(sems, per, n, before):
                for c in range(n):
                    dve.wait_ge(sems["rstd"], nth(per, before, n, 0, c))
                    for j in range(TPG):
                        w = slice(j * P, (j + 1) * P)
                        last = dve.tensor_scalar(X1[c][:, w], X[c][:, w], mv[c][:, 0, j, 0:1], rs[c][:, 0, j:j + 1], ALU.subtract, ALU.mult)
                    last.then_inc(sems["x1"], 1)

            def softplus(sems, per, k, n, before, bank0, bias, to, done="sp"):
                for c in range(n):
                    dve.wait_ge(sems["exp"], nth(per, before, n, k, c))
                    dve.tensor_scalar(EL[c], EL[c], CAP, None, ALU.min).then_inc(sems["capped"], 1)
                for c in range(n):
                    dve.wait_ge(sems["log"], nth(per, before, n, k, c))
                    if bias is None:
                        ins = dve.tensor_tensor(to(c), bank[:, bank0 + c, :], EL[c], ALU.max)
                    else:
                        ins = dve.scalar_tensor_tensor(out=to(c), in0=bank[:, bank0 + c, :], scalar=cols[:, bias:bias + 1], in1=EL[c],
                                                       op0=ALU.add, op1=ALU.max)
                    ins.then_inc(sems[done], 1)

            def dve_msg(kind, n, grp, before, used):
                for c in range(n):
                    rows = bass.ds((grp + c) * GW, GW)
                    dve.scalar_tensor_tensor(out=X[c], in0=G[:, rows], scalar=0.5, in1=row_buf[:, rows], op0=ALU.mult, op1=ALU.add).then_inc(ms["v"], 1)
                ln_stats(ms, 1, 0, n, before, X, lambda c: dve.wait_ge(ms["v"], nth(1, before, n, 0, c)))
                normalise(ms, 1, n, before)
                dve.wait_ge(ms["g"], nth(1, before, n, 0, n - 1))
                softplus(ms, 1, 0, n, before, HB, None, lambda c: H[c])
                for c in range(n):
                    dve.wait_ge(ms["sp"], nth(1, before, n, 0, c))
                    dve.tensor_tensor(G[:, bass.ds((grp + c) * GW, GW)], bank[:, U + c, :], H[c], ALU.mult).then_inc(ms["msg"], 1)

            DVE_OPS = in_turn([(0, "v"), (0.6, "stats 1"), (2.5, "x1"), (39.2, "stats 2"), (42, "nmean")]
                              + [(FIRST_T + STEP_T * k + 0.5, ("cap", k)) for k in range(NSTEP)]
                              + [(FIRST_T + STEP_T * k + 2, ("max", k)) for k in range(NSTEP)])

            def row_stats(c, k, use, rows):
                for j in range(TPG):
                    last = dve.bn_stats(stats[c][:, j, :], rows[:, j * P:(j + 1) * P])
                last.then_inc(dve_done[c], 1)
                dve.wait_ge(dve_done[c], after(DVE_STEPS, use, f"stats {k + 1}"))
                dve.memset(tick[:], 0.0)
                for j in range(TPG):
                    last = dve.bn_aggr(mv[c][:, k, j, :], stats[c][:, j, :])
                last.then_inc(dve_done[c], 1)
                dve.wait_ge(dve_done[c], after(DVE_STEPS, use, f"mean {k + 1}"))
                dve.tensor_scalar(ve[c][:, k, :], mv[c][:, k, :, 1], EPS if k else EPS / 4, None, ALU.add).then_inc(dve_done[c], 1)

            def dve_window(w, kind):
                for op, c, lag in DVE_OPS:
                    of, use = group_kind(w, c, lag, kind), w - lag
                    if of is None:
                        continue
                    edge_rows = None if of == "node" else bass.ds((use * CHAINS + c - NG) * GW, GW)
                    if op == "v":
                        if of == "edge":
                            dve.wait_ge(x_arrived[c], (use + 1) * 16)
                            dve.scalar_tensor_tensor(out=X[c], in0=X[c], scalar=0.5, in1=row_buf[:, edge_rows],
                                                     op0=ALU.mult, op1=ALU.add).then_inc(edge_v, 1)
                    elif op == "stats 1":
                        if of == "edge":
                            dve.wait_ge(edge_v, use * CHAINS + (c - NG + 1))
                        else:
                            dve.wait_ge(x_arrived[c], (use + 1) * 16)
                        row_stats(c, 0, use, X[c])
                    elif op == "x1":
                        dve.wait_ge(pool_done[c], after(POOL_STEPS, use, "rstd 1"))
                        if later(use):
                            dve.wait_ge(pe_done[c], after(PE_STEPS, use - 1, "y"))
                        for j in range(TPG):
                            cw = slice(j * P, (j + 1) * P)
                            last = dve.tensor_scalar(X1[c][:, cw], X[c][:, cw], mv[c][:, 0, j, 0:1], rs[c][:, 0, j:j + 1], ALU.subtract, ALU.mult)
                        last.then_inc(dve_done[c], 1)
                    elif op == "stats 2":
                        dve.wait_ge(pe_done[c], after(PE_STEPS, use, "y"))
                        row_stats(c, 1, use, bank[:, HB + c, :])
                    elif op == "nmean":
                        dve.wait_ge(pool_done[c], after(POOL_STEPS, use, "rstd 2"))
                        dve.scalar_tensor_tensor(out=nm[c][:], in0=mv[c][:, 1, :, 0], scalar=-1.0, in1=rs[c][:, 1, :],
                                                 op0=ALU.mult, op1=ALU.mult).then_inc(dve_done[c], 1)
                    elif op[0] == "cap":
                        dve.wait_ge(act_done[c], after(ACT_STEPS, use, ("exp", op[1])))
                        dve.tensor_scalar(EL[c], EL[c], CAP, None, ALU.min).then_inc(dve_done[c], 1)
                    else:
                        k = op[1]
                        bank0, bias, _ = STEPS[k]
                        if k == (of == "node") and later(use):
                            stored = use * 16 if of == "node" else (use - NODE_USES[c]) * (16 * TPG) + 16 * NODE_USES[c]
                            dve.wait_ge(out_stored[c], stored)
                        dve.wait_ge(act_done[c], after(ACT_STEPS, use, ("ln", k)))
                        to = bank[:, U + c, :] if k == 0 and of == "node" else H[c]
                        done = edge_u0 if k == 0 and of == "edge" else dve_done[c]
                        if bias is None:
                            dve.tensor_tensor(to, bank[:, bank0 + c, :], EL[c], ALU.max).then_inc(done, 1)
                        else:
                            dve.scalar_tensor_tensor(out=to, in0=bank[:, bank0 + c, :], scalar=cols[:, bias:bias + 1], in1=EL[c],
                                                     op0=ALU.add, op1=ALU.max).then_inc(done, 1)
                        if k == 0 and of == "edge":
                            dve.wait_ge(edge_u0, use * CHAINS + (c - NG + 1))
                            dve.tensor_tensor(bank[:, U + c, :], H[c], G[:, edge_rows], ALU.add).then_inc(dve_done[c], 1)

            for k in range(3):
                segment_sums(k)
            dve.wait_ge(tot_gathered[2], 16 * ET)
            dve.wait_ge(seg_mm, 2 * EG * 3)
            each_run(dve, msg_runs, dve_msg)
            dve.wait_ge(ms["msg"], EG)
            segment_sums(3)
            dve.wait_ge(xs_gathered, 16 * ET)
            dve.wait_ge(seg_rows, 2 * EG * 4)
            each_window(dve, dve_window)


_INS = ["x", "src", "dst", "edge_attr_64", "edge_weight", "L1_gnn_Wg", "L1_gnn_Wi", "L1_gnn_bi", "L1_gnn_Wj", "L1_gnn_bj",
        "L1_gnn_Wv", "L1_gnn_bv", "L1_gnn_gate", "L1_gnn_res_W1", "L1_gnn_res_b1", "L1_gnn_res_W2", "L1_gnn_res_b2"]


def kernel(**inputs):
    import numpy as _np
    import concourse.bacc as _bacc
    from concourse import mybir as _mybir
    from concourse.bass_utils import run_bass_kernel_spmd as _run

    nc = _bacc.Bacc("TRN2", target_bir_lowering=False, num_devices=1)
    arrays, args = {}, []
    for name in _INS:
        a = _np.ascontiguousarray(inputs[name])
        arrays[f"in_{name}"] = a
        args.append(nc.dram_tensor(f"in_{name}", a.shape, _mybir.dt.from_np(a.dtype), kind="ExternalInput").ap())
    out = nc.dram_tensor("out_0", arrays["in_x"].shape, _mybir.dt.float32, kind="ExternalOutput").ap()
    gnn_kernel(nc, *args, out)
    r = _run(nc, [arrays], core_ids=[0])
    return r.results[0]["out_0"]
```

```python
from contextlib import ExitStack

import concourse.bass as bass
from concourse import mybir

ALU = mybir.AluOpType
ACT = mybir.ActivationFunctionType
F32 = mybir.dt.float32
BF16 = mybir.dt.bfloat16
I32 = mybir.dt.int32

P = 128
TPG = 4
GW = TPG * P
DIG = 256
CHAINS = 4
CAP = 2.0 ** 63
EPS = 1e-05
FAR = 100000.0


def plan(n_groups):
    runs, full = [], n_groups // CHAINS
    if full:
        runs.append((1, CHAINS, 0))
        runs.append((full - 1, CHAINS, CHAINS))
    if n_groups % CHAINS:
        runs.append((1, n_groups % CHAINS, full * CHAINS))
    return runs


def gnn_kernel(nc, x, src, dst, attr, weight, Wg, Wi, bi, Wj, bj, Wv, bv, gate, W1, b1, W2, b2, out):
    N, F = x.shape
    E, R = attr.shape
    RES = W1.shape[0]
    assert F == P and N < DIG * DIG and RES == 3
    ET = -(-E // GW) * TPG
    EP = ET * P
    EG = ET // TPG
    FULLT, TAIL = E // P, E % P
    NG = -(-N // GW)
    ZROW = EP
    PW = 4 + R

    def dram(name, shape, dt):
        return nc.dram_tensor(name, shape, dt, kind="Internal").ap()

    ptr_table = dram("ptr_table", (2 * P * DIG, 1), I32)
    sorted_rows = dram("sorted_rows", (EP, PW), F32)
    sorted_src = dram("sorted_src", (ET, P), F32)
    totals = [dram(f"totals{k}", (EP + 1, F), F32) for k in range(3)]

    with ExitStack() as ctx:
        def sb(name, shape, dt=F32):
            return ctx.enter_context(nc.sbuf_tensor(name, shape, dt))

        def sem(name):
            return ctx.enter_context(nc.semaphore(name))

        bank = ctx.enter_context(nc.psum_tensor("bank", [P, 8, GW], F32))

        ident = sb("ident", [P, P])
        ones_bf = sb("ones_bf", [P, P], BF16)
        mats = {"Wi": Wi, "Wj": Wj, "Wv": Wv}
        for k in range(RES):
            mats[f"W1_{k}"] = W1[k]
            mats[f"W2_{k}"] = W2[k]
        order = list(mats)
        masks = sb("masks", [P, 2 * EP], BF16)
        seg_mask, open_mask = masks[:, 0:EP], masks[0:ET, EP:2 * EP]
        setup_space, at_s = masks[:].bitcast(F32), [ET * PW]

        def carve_s(shape, dt=F32):
            words = shape[1] * (shape[2] if len(shape) > 2 else 1)
            v = setup_space[0:shape[0], at_s[0]:at_s[0] + words]
            at_s[0] += words
            v = v if dt == F32 else v.bitcast(dt)
            return v.rearrange("p (a b) -> p a b", b=shape[2]) if len(shape) > 2 else v

        below = carve_s([P, P])
        shift_up = carve_s([P, P])
        wrap = carve_s([P, P])
        col_minus_row = carve_s([P, P])
        row_no = carve_s([P, P])
        earlier = carve_s([P, P])
        ones = carve_s([P, P])
        hi_no = carve_s([P, 2])
        w_nat = carve_s([P, len(order), P])
        wT = sb("wT", [P, len(order), P])
        wg_nat = carve_s([P, 2, P])
        wgT = sb("wgT", [P, 2, P])
        gate_diag = sb("gate_diag", [P, P])
        cols = sb("cols", [P, 12])
        C_BI, C_GATE, C_B1, C_B2, C_SUM = 0, 1, 2, 2 + RES, 2 + 2 * RES
        bias3 = sb("bias3", [3, 2, GW], BF16)
        row_buf = sb("row_buf", [P, EP])
        G = sb("G", [P, EP])
        rows_nat = carve_s([P, 2, P], I32)
        w_rows = carve_s([P, P])
        rows_f = carve_s([P, 4, P])
        rows_i = carve_s([P, 2, P], I32)
        e_cols = carve_s([P, 5, ET])
        meta = sb("meta", [P, ET, 4])
        out_idx = sb("out_idx", [P, ET], I32)
        src_rows = row_buf[:].bitcast(I32)
        payload = masks[:].bitcast(F32)[:, 0:ET * PW].rearrange("p (t w) -> p t w", w=PW)
        payload_i = masks[:].bitcast(I32)[:, 0:ET * PW].rearrange("p (t w) -> p t w", w=PW)
        meta_i = meta[:].rearrange("p t w -> p (t w)").bitcast(I32).rearrange("p (t w) -> p t w", w=4)

        at = [0]

        def carve(words, dt=F32):
            v = G[:, at[0]:at[0] + words]
            at[0] += words
            return v if dt == F32 else v.bitcast(dt)

        oh_hi, oh_lo = ([[carve(DIG // 2, BF16) for _ in range(TPG)] for _ in range(2)] for _ in range(2))
        hi_row = [carve(GW, I32) for _ in range(2)]
        oh_hiT = [[carve(GW) for _ in range(2)] for _ in range(2)]
        acc_a, acc_b = carve(TPG), carve(TPG)
        cum = [carve(2 * DIG) for _ in range(2)]
        hist, incl, base, ptr_f = (carve(2 * DIG) for _ in range(4))
        zeros = carve(DIG)
        offs = carve(2)
        ptr_i = carve(2 * DIG, I32)
        digits = carve(DIG // 2, BF16)
        dst_idx, pos_idx = carve(ET, I32), carve(ET, I32)
        pos, same_next = carve(ET), carve(ET)
        tile_before = carve(P)
        srcT = carve(P)
        src_s = carve(ET + 1)
        zero_row = carve(P)[0:1, :]
        brow = carve(2 * 3 * P)[0:1, :].rearrange("o (a b f) -> o a b f", a=2, b=3)
        bpart = carve(3 * TPG * P, BF16)[0:1, :].rearrange("o (a b r f) -> o a b r f", a=2, b=3, r=TPG)

        seg_m = sb("seg_m", [P, GW])
        open_sums = seg_m[0:ET, 5 * P // 2:7 * P // 2]
        open_parts = seg_m[0:ET, P:5 * P // 2].bitcast(BF16).rearrange("t (a f) -> t a f", a=3)

        seg_M = [[sb(f"seg_M{s}{h}", [P, 2 * P]) for h in range(2)] for s in range(2)]

        X, X1, S, EL, H = ([sb(f"{q}{c}", [P, GW])[:] for c in range(CHAINS)] for q in ("X", "X1_", "S", "EL", "H"))
        junk, same = ([X1[j][:, a:b] for j in range(TPG)] for a, b in ((0, DIG), (DIG, DIG + P)))
        attr_in = [seg_m[:, 0:2 * P], seg_m[:, 2 * P:GW], seg_M[0][0][:], seg_M[0][1][:]]
        attrT = [H[c][:, 0:2 * P] for c in range(CHAINS)]
        zeros_w = carve_s([P, P])
        zeros_r = carve_s([P, GW])
        tick = sb("tick", [P, 1])
        stats = [(sb(f"stats{c}", [P, TPG, 6])[:], EL[c][:, 0:6 * TPG].rearrange("p (j w) -> p j w", w=6)) for c in range(CHAINS)]
        mv = [sb(f"mv{c}", [P, 2, TPG, 2]) for c in range(CHAINS)]
        ve = [sb(f"ve{c}", [P, 2, TPG]) for c in range(CHAINS)]
        rs = [sb(f"rs{c}", [P, 2, TPG]) for c in range(CHAINS)]
        nm = [sb(f"nm{c}", [P, TPG]) for c in range(CHAINS)]
        minus_half = sb("minus_half", [P, TPG])

        iotas, consts = sem("iotas"), sem("consts")
        w_loaded, b_loaded = sem("w_loaded"), sem("b_loaded")
        wT_psum, wT_ready = sem("wT_psum"), sem("wT_ready")
        bias_parts, bias_ready = sem("bias_parts"), sem("bias_ready")
        pads_set, rows_loaded, row_bcast = sem("pads_set"), sem("rows_loaded"), sem("row_bcast")
        attr_loaded = sem("attr_loaded")
        rows_split, cols_psum = sem("rows_split"), sem("cols_psum")
        idx_ready = sem("idx_ready")
        onehot_ready, hist_added = sem("onehot_ready"), sem("hist_added")
        scan_ready, offs_psum, ptr_ready, ptr_stored = sem("scan_ready"), sem("offs_psum"), sem("ptr_ready"), sem("ptr_stored")
        tile_onehots, onehotT_ready = sem("tile_onehots"), sem("onehotT_ready")
        cum_copied, cum_added, place_psum, place_read = sem("cum_copied"), sem("cum_added"), sem("place_psum"), sem("place_read")
        pos_ready, ptr_gathered, payload_set, scattered = sem("pos_ready"), sem("ptr_gathered"), sem("payload_set"), sem("scattered")
        meta_loaded, meta_split, near_psum = sem("meta_loaded"), sem("meta_split"), sem("near_psum")
        srcT_stored, srow_loaded, masks_ready = sem("srcT_stored"), sem("srow_loaded"), sem("masks_ready")
        zero_stored = sem("zero_stored")
        xd_gathered = sem("xd_gathered")
        tot_gathered = [sem(f"tot_gathered{k}") for k in range(3)]
        seg_in, near_read = sem("seg_in"), sem("near_read")
        seg_expanded, seg_mm, seg_taken = ([sem(f"seg_{q}{h}") for h in range(2)] for q in ("expanded", "mm", "taken"))
        open_copied, open_T, open_loaded, open_split = sem("open_copied"), sem("open_T"), sem("open_loaded"), sem("open_split")
        tot_stored = sem("tot_stored")
        xs_gathered = sem("xs_gathered")
        link_sem, hi_split, places_added = sem("link"), sem("hi_split"), sem("places_added")
        srcT_ready, wg_zeroed = sem("srcT_ready"), sem("wg_zeroed")

        ms = {k: sem(f"msg_{k}") for k in
              ("v", "stats", "mean", "var", "rstd", "x1", "xT", "exp_s", "s", "lin", "exp", "capped", "log", "sp",
               "attrT", "attr_copied", "g", "msg")}
        act_done, dve_done, pe_done, pool_done = ([sem(f"{e}_done{c}") for c in range(CHAINS)] for e in ("act", "dve", "pe", "pool"))
        dve_front, pool_front = ([sem(f"{e}_front{c}") for c in range(CHAINS)] for e in ("dve", "pool"))
        edge_v, edge_u0 = sem("edge_v"), sem("edge_u0")
        attr_arrived = [sem(f"attr_arrived{c}") for c in range(CHAINS)]
        x_arrived = [sem(f"x_arrived{c}") for c in range(CHAINS)]
        out_stored = [sem(f"out_stored{c}") for c in range(CHAINS)]

        def runs_of(kinds):
            runs, before, used = [], 0, [0] * CHAINS
            for kind, count in kinds:
                for reps, n, first in plan(count):
                    runs.append((kind, reps, n, first, before, list(used)))
                    before += reps * n
                    for c in range(n):
                        used[c] += reps
            return runs, used

        msg_runs, _ = runs_of([("msg", EG)])

        GROUPS = NG + EG
        U, HB = 0, 4
        SEG_BANK = (U, HB)
        STEPS = [(U, C_BI, None)]
        for r in range(RES):
            STEPS.append((U, C_SUM + r - 1 if r else None, 3 + 2 * r))
            STEPS.append((HB, C_B1 + r, 4 + 2 * r))
        STEPS.append((U, C_SUM + RES - 1, 2))
        NSTEP = len(STEPS)
        LINS = NSTEP - 1
        SOFTPLUS = range(NSTEP)
        ACT_STEPS = ["exp s", "ln s"] + [(q, k) for k in SOFTPLUS for q in ("exp", "ln")] + ["norm"]
        DVE_FRONT = ["stats 1", "mean 1", "var 1", "x1"]
        DVE_STEPS = [(q, k) for k in SOFTPLUS for q in ("cap", "max")] + ["stats 2", "mean 2", "var 2", "nmean"]
        PE_STEPS = ["xT"] + [("lin", k) for k in range(LINS)] + ["y"]
        POOL_FRONT = ["rstd 1"]
        POOL_STEPS = ["rstd 2"]

        def after(steps, use, step):
            return use * len(steps) + (steps.index(step) + 1)

        WINDOW = 50
        START = (0, 12.5, 25.0, 37.5)
        DUE = {"v": 37.8, "stats 1": 38.1, "mean 1": 46.1, "var 1": 46.2, "rstd 1": 43.2, "x1": 49.0,
               "xT": 50.3, "exp s": 50.0, "ln s": 52.5, ("lin", 0): 55.0,
               ("exp", 0): 54.5, ("exp", 1): 58.0, ("exp", 2): 61.6, ("exp", 3): 66.2, ("exp", 4): 70.5, ("exp", 5): 75.5, ("exp", 6): 80.4, ("exp", 7): 84.1,
               ("cap", 0): 54.8, ("cap", 1): 58.3, ("cap", 2): 62.2, ("cap", 3): 64.9, ("cap", 4): 72.6, ("cap", 5): 75.9, ("cap", 6): 80.7, ("cap", 7): 86.0,
               ("ln", 0): 57.5, ("ln", 1): 58.6, ("ln", 2): 64.3, ("ln", 3): 67.2, ("ln", 4): 71.6, ("ln", 5): 77.2, ("ln", 6): 82.6, ("ln", 7): 85.4,
               ("max", 0): 57.4, ("max", 1): 60.3, ("max", 2): 64.0, ("max", 3): 68.1, ("max", 4): 73.7, ("max", 5): 77.4, ("max", 6): 82.9, ("max", 7): 86.8,
               ("lin", 1): 60.7, ("lin", 2): 67.0, ("lin", 3): 69.6, ("lin", 4): 74.7, ("lin", 5): 80.6, ("lin", 6): 83.0,
               "y": 88.5, "stats 2": 89.9, "mean 2": 92.0, "var 2": 92.9,
               "rstd 2": 91.5, "nmean": 95.6, "norm": 97.1, "store": 93.3}

        def in_turn(ops):
            placed = []
            for op in ops:
                for c in range(CHAINS):
                    t = DUE[op] + START[c]
                    placed.append((t % WINDOW, c, int(t // WINDOW), op))
            return [(t, op, c, lag) for t, c, lag, op in sorted(placed, key=lambda q: q[:2])]

        MOVE_W = 3
        SORT_W = MOVE_W + 1
        MSG_USE = SORT_W + 4 * MOVE_W
        LAGS = 2
        LAST_W = (GROUPS - 1) // CHAINS + LAGS
        NODE_W, EDGE_W = NG // CHAINS, -(-NG // CHAINS)
        LAYER_W = [SORT_W + MOVE_W * (k + 1) for k in range(3)]
        PLAN = ([("windows", [0, 1, 2, (3, SORT_W)]), ("near",)]
                + [step for k in range(3) for step in (("windows", [(LAYER_W[k] - MOVE_W, LAYER_W[k])]), ("seg", k))]
                + [("windows", [(LAYER_W[2], MSG_USE)] + list(range(MSG_USE, MSG_USE + LAGS))), ("messages",), ("seg", 3)]
                + [("windows", [MSG_USE, MSG_USE + 1, (MSG_USE + LAGS, NODE_W)] + list(range(NODE_W, EDGE_W + LAGS))
                    + [(EDGE_W + LAGS, GROUPS // CHAINS)] + list(range(GROUPS // CHAINS, LAST_W + 1)))])

        def follow_plan(eng, window, near, seg, messages):
            uses = (0, MSG_USE)
            for what, *arg in PLAN:
                if what == "windows":
                    for w in arg[0]:
                        if isinstance(w, int):
                            window(w, None, uses)
                        else:
                            with eng.Fori(*w) as one:
                                window(one, "node" if w[1] <= NODE_W else "edge", uses)
                elif what == "near":
                    near()
                elif what == "seg":
                    seg(arg[0])
                else:
                    messages()
                    uses = (MSG_USE, LAST_W + 1)

        def group_kind(w, c, lag, kind, uses):
            if kind:
                return kind
            i = (w - lag) * CHAINS + c
            return None if not uses[0] <= w - lag < uses[1] or i >= GROUPS else "node" if i < NG else "edge"

        def node_row(i):
            return min(i * GW, N - GW) if isinstance(i, int) else i * GW

        NODE_USES = [len(range(c, NG, CHAINS)) for c in range(CHAINS)]

        def each_run(eng, runs, body):
            for kind, reps, n, first, before, used in runs:
                if reps > 1:
                    with eng.Fori(0, reps) as g:
                        body(kind, n, g * n + first, g * n + before, [g + u for u in used])
                else:
                    body(kind, n, first, before, used)

        def nth(before, n, c):
            return before + (c + 1)

        def over_groups(eng, body):
            body(0)
            with eng.Fori(1, EG) as g:
                body(g)

        assert EG % 2

        def by_twos(eng, first, end, body):
            assert (end - first) % 2 == 0
            with eng.Fori(0, (end - first) // 2) as pair:
                for i in range(2):
                    body(pair * 2 + (first + i), (first + i) % 2)

        def ahead_by_one(eng, ahead, body):
            def step(g, s):
                ahead(g + 1, 1 - s)
                body(g)

            ahead(0, 0)
            step(0, 0)
            step(1, 1)
            by_twos(eng, 2, EG - 1, step)
            body(EG - 1)

        def half(g, h):
            return bass.ds(g * GW + 2 * h * P, 2 * P)

        def expand(eng, scale, k, g, s, h):
            n = g + EG * 2 * k
            if not (isinstance(n, int) and n < 2):
                eng.wait_ge(seg_mm[h], n - 1)
            if k == 3:
                ins = scale(seg_M[s][h][:], seg_mask[:, half(g, h)], None)
            else:
                for j in range(2):
                    t = g * TPG + (2 * h + j)
                    ins = scale(seg_M[s][h][:, j * P:(j + 1) * P], seg_mask[:, bass.ds(t * P, P)], meta[:, bass.ds(t, 1), 3])
            ins.then_inc(seg_expanded[h], 1)

        def later(value):
            return not (isinstance(value, int) and value == 0)

        block = ctx.enter_context(nc.Block())

        @block.sync
        def _(sp):
            with nc.allow_non_contiguous_dma(reason="small columns"):
                for v, at_c in [(bi, C_BI), (gate, C_GATE)] + [(b1[k], C_B1 + k) for k in range(RES)] + [(b2[k], C_B2 + k) for k in range(RES)]:
                    sp.dma_start(cols[:, at_c:at_c + 1], v.rearrange("(p o) -> p o", o=1)).then_inc(b_loaded, 16)
            sp.dma_start(brow[:, 0, 0, :], bv.rearrange("(o f) -> o f", o=1)).then_inc(b_loaded, 16)
            sp.dma_start(brow[:, 1, 0, :], bj.rearrange("(o f) -> o f", o=1)).then_inc(b_loaded, 16)

            sp.wait_ge(pads_set, 5)
            for v, rows in ((src, rows_nat[:, 0, :]), (dst, rows_nat[:, 1, :]), (weight, w_rows[:])):
                sp.dma_start(rows[0:FULLT, :], v[0:FULLT * P].rearrange("(t p) -> t p", p=P)).then_inc(rows_loaded, 16)
                sp.dma_start(rows[FULLT:FULLT + 1, 0:TAIL], v[FULLT * P:E].rearrange("(o p) -> o p", o=1)).then_inc(rows_loaded, 16)
            sp.dma_start(src_rows[:, 0:E], src.rearrange("(o e) -> o e", o=1).to_broadcast([P, E])).then_inc(row_bcast, 16)
            sp.dma_start(payload[:, 0:FULLT, 4:PW], attr[0:FULLT * P].rearrange("(t p) f -> p t f", p=P)).then_inc(attr_loaded, 16)
            sp.dma_start(payload[0:TAIL, FULLT, 4:PW], attr[FULLT * P:E]).then_inc(attr_loaded, 16)
            sp.wait_ge(consts, 1)
            for k in range(3):
                sp.dma_start(totals[k][ZROW:ZROW + 1, :], zero_row).then_inc(zero_stored, 16)
            sp.wait_ge(bias_parts, 1)
            for part in range(3):
                for q in range(2):
                    sp.dma_start(bias3[part:part + 1, q, :], bpart[:, q, part, :, :].rearrange("o a b -> o (a b)")).then_inc(bias_ready, 16)

            sp.wait_ge(ptr_ready, 1)
            sp.dma_start(ptr_table.rearrange("(c p l) o -> p c (l o)", c=2, l=DIG), ptr_i.rearrange("p (c l) -> p c l", c=2)).then_inc(ptr_stored, 16)

            def store_totals(k):
                if k == 3:
                    return
                for h in range(2):
                    sp.wait_ge(seg_taken[h], EG * (2 * k + 1))
                sp.dma_start(open_sums, G[P - 1:P, :].rearrange("o (t f) -> o t f", f=F)).then_inc(open_loaded, 16)
                with sp.Fori(0, EG) as g:
                    for h in range(2):
                        sp.wait_ge(seg_taken[h], g + (EG * (2 * k + 1) + 1))
                    sp.dma_start(totals[k][bass.ds(g * GW, GW), :].rearrange("(j p) f -> p j f", p=P),
                                 G[:, bass.ds(g * GW, GW)].rearrange("p (j f) -> p j f", f=F)).then_inc(tot_stored, 16)

            def attr_loads(kind, n, grp, before, used):
                if later(before):
                    sp.wait_ge(ms["attrT"], before)
                for c in range(n):
                    sp.dma_start(attr_in[c].rearrange("p (j r) -> p j r", r=R),
                                 sorted_rows[bass.ds((grp + c) * GW, GW), :].rearrange("(j p) w -> p j w", p=P)[:, :, 4:PW]).then_inc(attr_arrived[c], 16)

            def message_loads():
                each_run(sp, msg_runs, attr_loads)
                sp.wait_ge(ms["x1"], EG)

            def node_loads(w, kind, uses):
                for c in range(CHAINS):
                    of = group_kind(w, c, 0, kind, uses)
                    if of is None:
                        continue
                    if later(w):
                        sp.wait_ge(dve_front[c], after(DVE_FRONT, w - 1, "x1"))
                    i = w * CHAINS + c
                    Xc = X[c].rearrange("p (j f) -> p j f", f=F)
                    if of == "node":
                        sp.dma_start(Xc, x[bass.ds(node_row(i), GW), :].rearrange("(p j) f -> p j f", j=TPG)).then_inc(x_arrived[c], 16)
                    else:
                        sp.dma_start(Xc, totals[2][bass.ds((i - NG) * GW, GW), :].rearrange("(j p) f -> p j f", p=P)).then_inc(x_arrived[c], 16)

            def sorted_back():
                sp.wait_ge(scattered, 16 * ET)
                with nc.allow_non_contiguous_dma(reason="four words of each row"):
                    sp.dma_start(meta[:], sorted_rows.rearrange("(t p) w -> p t w", p=P)[:, :, 0:4]).then_inc(meta_loaded, 16)
                sp.wait_ge(srcT_ready, 1)
                sp.dma_start(sorted_src, srcT[0:ET, :]).then_inc(srcT_stored, 16)
                sp.wait_ge(srcT_stored, 16)
                sp.dma_start(row_buf[:], sorted_src.rearrange("t p -> (t p)").rearrange("(o e) -> o e", o=1).to_broadcast([P, EP])).then_inc(srow_loaded, 16)

            follow_plan(sp, node_loads, sorted_back, store_totals, message_loads)

        @block.gpsimd
        def _(pool):
            exact = dict(allow_small_or_imprecise_dtypes=True)
            pool.iota(col_minus_row[:], [[1, P]], base=0, channel_multiplier=-1, **exact).then_inc(iotas, 1)
            pool.iota(row_no[:], [[0, P]], base=0, channel_multiplier=1, **exact).then_inc(iotas, 1)
            pool.iota(digits, [[1, DIG]], base=0, channel_multiplier=0, **exact).then_inc(iotas, 1)
            pool.iota(hi_no[:], [[P, 2]], base=0, channel_multiplier=1, **exact).then_inc(iotas, 1)
            pool.iota(rows_nat[:, 0, :], [[1, P]], base=N - E, channel_multiplier=P).then_inc(pads_set, 1)
            pool.memset(rows_nat[:, 1, :], 0).then_inc(pads_set, 1)
            pool.memset(w_rows[:], 0.0).then_inc(pads_set, 1)
            pool.iota(src_rows[:, E:EP], [[1, EP - E]], base=N, channel_multiplier=0).then_inc(pads_set, 1)
            pool.memset(payload[:, FULLT:ET, :], 0.0).then_inc(pads_set, 1)
            pool.memset(minus_half[:], -0.5).then_inc(iotas, 1)

            pool.wait_ge(ptr_stored, 16)
            pool.wait_ge(idx_ready, 1)
            pool.wait_ge(attr_loaded, 32)
            for t in range(ET):
                pool.indirect_dma_start(payload_i[:, t, 2:3], None, ptr_table,
                                        bass.IndirectOffsetOnAxis(ap=dst_idx[:, t:t + 1], axis=0)).then_inc(ptr_gathered, 16)
            pool.wait_ge(ptr_gathered, 16 * ET)
            pool.wait_ge(pos_ready, 1)
            pool.wait_ge(payload_set, 1)
            pool.wait_ge(zero_stored, 48)

            def move(what, t):
                if what == "sort":
                    pool.indirect_dma_start(sorted_rows, bass.IndirectOffsetOnAxis(ap=pos_idx[:, t:t + 1], axis=0),
                                            payload[:, t, :], None).then_inc(scattered, 16)
                elif what == "targets":
                    pool.indirect_dma_start(row_buf[:, t * P:(t + 1) * P], None, x,
                                            bass.IndirectOffsetOnAxis(ap=meta_i[:, t, 1:2], axis=0)).then_inc(xd_gathered, 16)
                elif what == "sources":
                    pool.indirect_dma_start(row_buf[:, t * P:(t + 1) * P], None, x,
                                            bass.IndirectOffsetOnAxis(ap=meta_i[:, t, 0:1], axis=0)).then_inc(xs_gathered, 16)
                else:
                    pool.indirect_dma_start(G[:, t * P:(t + 1) * P], None, totals[what],
                                            bass.IndirectOffsetOnAxis(ap=meta_i[:, t, 2:3], axis=0)).then_inc(tot_gathered[what], 16)

            def msg_rstd(kind, n, grp, before, used):
                for c in range(n):
                    pool.wait_ge(ms["var"], nth(before, n, c))
                    pool.tensor_tensor(rs[c][:, 0, :], ve[c][:, 0, :], minus_half[:], ALU.pow).then_inc(ms["rstd"], 1)

            POOL_OPS = in_turn(POOL_FRONT + POOL_STEPS + ["store"])

            moved = [0]

            def pool_window(w, kind, uses, what=None, first=0, end=0):
                for t, op, c, lag in POOL_OPS:
                    while what is not None and moved[0] < ET and moved[0] * (end - first) * WINDOW < ET * ((w - first) * WINDOW + t):
                        move(what, moved[0])
                        moved[0] += 1
                    of, use = group_kind(w, c, lag, kind, uses), w - lag
                    if of is None:
                        continue
                    if op == "rstd 1":
                        pool.wait_ge(dve_front[c], after(DVE_FRONT, use, "var 1"))
                        pool.tensor_tensor(rs[c][:, 0, :], ve[c][:, 0, :], minus_half[:], ALU.pow).then_inc(pool_front[c], 1)
                    elif op == "rstd 2":
                        pool.wait_ge(dve_done[c], after(DVE_STEPS, use, "var 2"))
                        pool.tensor_tensor(rs[c][:, 1, :], ve[c][:, 1, :], minus_half[:], ALU.pow).then_inc(pool_done[c], 1)
                    elif of == "node":
                        pool.wait_ge(act_done[c], after(ACT_STEPS, use, "norm"))
                        i = use * CHAINS + c
                        if isinstance(i, int) and i == NG - 1:
                            pool.wait_ge(out_stored[(i - 1) % CHAINS], 16 * ((i - 1) // CHAINS + 1))
                        pool.dma_start(out[bass.ds(node_row(i), GW), :].rearrange("(p j) f -> p j f", j=TPG),
                                       H[c].rearrange("p (j f) -> p j f", f=F)).then_inc(out_stored[c], 16)
                    else:
                        i = use * CHAINS + c - NG
                        if i == 0:
                            for other in range(CHAINS):
                                pool.wait_ge(out_stored[other], 16 * NODE_USES[other])
                        pool.wait_ge(act_done[c], after(ACT_STEPS, use, "norm"))
                        for j in range(TPG):
                            pool.indirect_dma_start(out, bass.IndirectOffsetOnAxis(ap=out_idx[:, i * TPG + j:i * TPG + j + 1], axis=0),
                                                    H[c][:, j * P:(j + 1) * P], None,
                                                    bounds_check=N - 1, oob_is_err=False).then_inc(out_stored[c], 16)

            def windows_and_moves(first, end, uses, what):
                moved[0] = 0
                for w in range(first, end):
                    start = first + (0.8 if first in (0, MSG_USE) else 0)
                    pool_window(w, None, uses, what, start, end)
                for t in range(moved[0], ET):
                    move(what, t)

            early, late = (0, MSG_USE), (MSG_USE, LAST_W + 1)
            windows_and_moves(0, SORT_W, early, "sort")
            pool.wait_ge(masks_ready, EG)
            windows_and_moves(SORT_W, SORT_W + MOVE_W, early, "targets")
            for k in range(3):
                pool.wait_ge(tot_stored, 16 * EG * (k + 1))
                windows_and_moves(LAYER_W[k], LAYER_W[k] + MOVE_W, early, k)
            for w in range(MSG_USE, MSG_USE + LAGS):
                pool_window(w, None, early)
            each_run(pool, msg_runs, msg_rstd)
            pool.wait_ge(ms["v"], EG)
            windows_and_moves(MSG_USE, MSG_USE + SORT_W, late, "sources")
            with pool.Fori(MSG_USE + SORT_W, NODE_W) as w:
                pool_window(w, "node", late)
            for w in range(NODE_W, LAST_W + 1):
                pool_window(w, None, late)
            for c in range(CHAINS):
                edge_uses = len(range(c, GROUPS, CHAINS)) - NODE_USES[c]
                pool.wait_ge(out_stored[c], 16 * NODE_USES[c] + 16 * TPG * edge_uses)

        def act_msg(kind, n, grp, before, used):
            act = nc.scalar
            for c in range(n):
                act.wait_ge(ms["attrT"], nth(before, n, c))
                act.copy(attrT[c], bank[:, c, 0:2 * P]).then_inc(ms["attr_copied"], 1)
            for c in range(n):
                act.wait_ge(ms["xT"], nth(before, n, c))
                act.activation(EL[c], bank[:, HB + c, :], ACT.Exp).then_inc(ms["exp_s"], 1)
            for c in range(n):
                act.wait_ge(ms["exp_s"], nth(before, n, c))
                act.activation(S[c], EL[c], ACT.Ln, bias=1.0).then_inc(ms["s"], 1)
            for c in range(n):
                act.wait_ge(ms["lin"], nth(before, n, c))
                act.activation(EL[c], bank[:, HB + c, :], ACT.Exp).then_inc(ms["exp"], 1)
            for c in range(n):
                act.wait_ge(ms["capped"], nth(before, n, c))
                act.activation(EL[c], EL[c], ACT.Ln, bias=1.0).then_inc(ms["log"], 1)

        ACT_OPS = in_turn(ACT_STEPS)

        def act_window(w, kind, uses):
            act = nc.scalar
            for _, op, c, lag in ACT_OPS:
                of, use = group_kind(w, c, lag, kind, uses), w - lag
                if of is None:
                    continue
                if op == "exp s":
                    act.wait_ge(pe_done[c], after(PE_STEPS, use, "xT"))
                    act.activation(EL[c], bank[:, HB + c, :], ACT.Exp).then_inc(act_done[c], 1)
                elif op == "ln s":
                    act.wait_ge(act_done[c], after(ACT_STEPS, use, "exp s"))
                    act.activation(S[c], EL[c], ACT.Ln, bias=1.0).then_inc(act_done[c], 1)
                elif op == "norm":
                    act.wait_ge(dve_done[c], after(DVE_STEPS, use, "nmean"))
                    for j in range(TPG):
                        cw = slice(j * P, (j + 1) * P)
                        last = act.activation(H[c][:, cw], bank[:, HB + c, cw], ACT.Identity, bias=nm[c][:, j:j + 1], scale=rs[c][:, 1, j:j + 1])
                    last.then_inc(act_done[c], 1)
                elif op[0] == "exp":
                    k = op[1]
                    bank0, bias, _ = STEPS[k]
                    if k == 1:
                        act.wait_ge(dve_done[c], after(DVE_STEPS, use, ("max", 0)))
                    else:
                        act.wait_ge(pe_done[c], after(PE_STEPS, use, ("lin", max(k - 1, 0))))
                    if bias is None:
                        act.activation(EL[c], bank[:, bank0 + c, :], ACT.Exp).then_inc(act_done[c], 1)
                    else:
                        act.activation(EL[c], bank[:, bank0 + c, :], ACT.Exp, bias=cols[:, bias:bias + 1]).then_inc(act_done[c], 1)
                else:
                    act.wait_ge(dve_done[c], after(DVE_STEPS, use, ("cap", op[1])))
                    act.activation(EL[c], EL[c], ACT.Ln, bias=1.0).then_inc(act_done[c], 1)

        @block.scalar
        def _(act):
            act.preload_act_table_set("natural_log_exp_and_others")
            for i, name in enumerate(order):
                act.dma_start(w_nat[:, i, :], mats[name]).then_inc(w_loaded, 16)
            act.wait_ge(wg_zeroed, 1)
            for i in range(2):
                act.dma_start(wg_nat[:, i, i * R:(i + 1) * R], Wg).then_inc(w_loaded, 16)
            act.wait_ge(wT_psum, 1)
            act.copy(wT[:, 0:TPG, :], bank[:, 0, :].rearrange("p (j f) -> p j f", f=P)).then_inc(wT_ready, 1)
            act.copy(wT[:, TPG:2 * TPG, :], bank[:, 1, :].rearrange("p (j f) -> p j f", f=P)).then_inc(wT_ready, 1)
            act.copy(wT[:, 2 * TPG, :], bank[:, 2, 0:P]).then_inc(wT_ready, 1)
            act.copy(wgT[:], bank[:, 3, 0:2 * P].rearrange("p (i f) -> p i f", f=P)).then_inc(wT_ready, 1)

            def copy_counts(g):
                for j in range(TPG):
                    act.wait_ge(cum_added, g * TPG + j + 1)
                    if later(g) or j > 1:
                        act.wait_ge(place_psum, g * TPG + j - 1)
                    act.copy(cum[j % 2], bank[:, 0, :]).then_inc(cum_copied, 1)

            over_groups(act, copy_counts)

            def act_scale(to, mask, weight):
                return act.copy(to, mask) if weight is None else act.activation(to, mask, ACT.Copy, scale=weight)

            def act_seg(k):
                if k == 0:
                    act.wait_ge(masks_ready, EG)

                def take(g):
                    for h in range(2 if k == 3 else 1):
                        act.wait_ge(seg_mm[h], g + (EG * 2 * k + 1))
                        act.copy(G[:, half(g, h)], bank[:, SEG_BANK[h], 0:2 * P]).then_inc(seg_taken[h], 1)

                ahead_by_one(act, lambda g, s: expand(act, act_scale, k, g, s, 0), take)

            def act_messages():
                for c in range(CHAINS):
                    act.wait_ge(out_stored[c], 16 * MSG_USE)
                each_run(act, msg_runs, act_msg)

            follow_plan(act, act_window, lambda: None, act_seg, act_messages)

        @block.tensor
        def _(pe):
            pe.wait_ge(consts, 1)
            pe.wait_ge(w_loaded, 16 * (len(order) + 2))
            for i in range(len(order)):
                pe.transpose(bank[:, i // TPG, (i % TPG) * P:(i % TPG + 1) * P], w_nat[:, i, :], ident[:])
            for i in range(2):
                mm = pe.transpose(bank[:, 3, i * P:(i + 1) * P], wg_nat[:, i, :], ident[:])
            mm.then_inc(wT_psum, 1)

            pe.wait_ge(rows_split, 1)
            pe.wait_ge(wT_ready, 4)
            for q in range(4):
                pe.transpose(bank[:, 4, q * P:(q + 1) * P], rows_f[:, q, :], ident[:])
            pe.transpose(bank[:, 5, 0:P], w_rows[:], ident[:]).then_inc(cols_psum, 1)

            pe.matmul(bank[:, 0, :], zeros_w[:], zeros_r[:], start=True, stop=False, skip_group_check=True)
            def count_edges(g, s):
                for j in range(TPG):
                    pe.wait_ge(onehot_ready, g * TPG + j + 1)
                    for c in range(2):
                        mm = pe.matmul(bank[:, 0, c * DIG:(c + 1) * DIG], oh_hi[s][j][:, c * P:(c + 1) * P], oh_lo[s][j],
                                       start=False, stop=True, skip_group_check=True)
                    mm.then_inc(hist_added, 1)

            count_edges(0, 0)
            by_twos(pe, 1, EG, count_edges)
            pe.wait_ge(scan_ready, 1)
            pe.matmul(bank[:, 1, 0:1], below[:], incl[:, DIG - 1:DIG], start=True, stop=True)
            pe.matmul(bank[:, 1, 1:2], below[:], incl[:, 2 * DIG - 1:2 * DIG], start=True, stop=False)
            pe.matmul(bank[:, 1, 1:2], ones[:], incl[:, DIG - 1:DIG], start=False, stop=True).then_inc(offs_psum, 1)

            pe.wait_ge(ptr_ready, 1)
            pe.matmul(bank[:, 0, :], ident[:], base, start=True, stop=False, skip_group_check=True).then_inc(cum_added, 1)
            def place_products(g, s):
                pe.wait_ge(onehotT_ready, g + 1)
                for j in range(TPG):
                    pe.wait_ge(cum_copied, g * TPG + j + 1)
                    pe.wait_ge(tile_onehots, g * TPG + j + 1)
                    for c in range(2):
                        mm = pe.matmul(bank[:, 0, c * DIG:(c + 1) * DIG], oh_hi[s][j][:, c * P:(c + 1) * P], oh_lo[s][j],
                                       start=False, stop=True, skip_group_check=True)
                    mm.then_inc(cum_added, 1)
                    if later(g):
                        pe.wait_ge(place_read, g * TPG + (j + 1 - TPG))
                    for c in range(2):
                        mm = pe.matmul(bank[:, 2 + j, 0:DIG], oh_hiT[s][c][:, j * P:(j + 1) * P], cum[j % 2][:, c * DIG:(c + 1) * DIG],
                                       start=(c == 0), stop=(c == 1))
                    mm.then_inc(place_psum, 1)

            place_products(0, 0)
            by_twos(pe, 1, EG, place_products)

            def near():
                pe.wait_ge(meta_split, 1)
                pe.wait_ge(act_done[0], after(ACT_STEPS, SORT_W - 2, "norm"))
                pe.matmul(bank[:, HB, P:P + ET], shift_up[:], src_s[:, 0:ET], start=True, stop=False, skip_group_check=True)
                pe.matmul(bank[:, HB, P:P + ET], wrap[:], src_s[:, 1:ET + 1], start=False, stop=True, skip_group_check=True)
                pe.transpose(bank[0:ET, U, 0:P], src_s[:, 0:ET], ident[:]).then_inc(near_psum, 1)
                pe.wait_ge(near_read, 1)

            def segment_products(k):
                def first_pass(g, s):
                    if k in (1, 2):
                        pe.wait_ge(seg_in, g + (EG * (k - 1) + 1))
                    for h in range(2):
                        n = g + EG * 2 * k
                        if k == 3:
                            pe.wait_ge(seg_in, g * 2 + (2 * EG + h + 1))
                        pe.wait_ge(seg_expanded[h], g + (EG * k + 1))
                        if later(n):
                            pe.wait_ge(seg_taken[h], n)
                        for j in range(2):
                            w = slice(j * P, (j + 1) * P)
                            t = slice((2 * h + j) * P, (2 * h + j + 1) * P)
                            rows = bass.ds(g * GW + (2 * h + j) * P, P)
                            m = (seg_m[:, t], seg_M[s][h][:, w]) if k == 3 else (seg_M[s][h][:, w], (G if k else row_buf)[:, rows])
                            mm = pe.matmul(bank[:, SEG_BANK[h], w], *m, start=True, stop=True)
                        mm.then_inc(seg_mm[h], 1)

                def second_pass(g):
                    for h in range(2):
                        pe.wait_ge(seg_taken[h], g + EG * (2 * k + 1))
                        if k == 3:
                            for part in range(3):
                                mm = pe.matmul(bank[:, SEG_BANK[h], 0:2 * P], open_parts[:, part, :], open_mask[:, half(g, h)],
                                               start=(part == 0), stop=(part == 2))
                        else:
                            for j in range(2):
                                for part in range(3):
                                    mm = pe.matmul(bank[:, SEG_BANK[h], j * P:(j + 1) * P], open_mask[:, bass.ds(g * GW + (2 * h + j) * P, P)],
                                                   open_parts[:, part, :], start=(part == 0), stop=(part == 2))
                        mm.then_inc(seg_mm[h], 1)

                if k < 3:
                    pe.wait_ge(act_done[0], after(ACT_STEPS, LAYER_W[k] - 2, "norm"))
                if k == 0:
                    pe.wait_ge(xd_gathered, 16 * ET)
                first_pass(0, 0)
                by_twos(pe, 1, EG, first_pass)
                if k == 3:
                    pe.wait_ge(open_copied, 1)
                    pe.transpose(bank[0:ET, U, 0:P], seg_m[:, 0:ET], ident[:]).then_inc(open_T, 1)
                pe.wait_ge(open_split, k + 1)
                with pe.Fori(0, EG) as g:
                    second_pass(g)
                for h in range(2):
                    pe.wait_ge(seg_taken[h], EG * 2 * (k + 1))

            def pe_msg(kind, n, grp, before, used):
                for c in range(n):
                    pe.wait_ge(attr_arrived[c], (used[c] + 1) * 16)
                    if later(before):
                        pe.wait_ge(ms["msg"], before)
                    for i in range(2):
                        mm = pe.transpose(bank[:, U + c, i * P:(i + 1) * P], attr_in[c][:, i * P:(i + 1) * P], ident[:])
                    mm.then_inc(ms["attrT"], 1)
                for c in range(n):
                    pe.wait_ge(ms["x1"], nth(before, n, c))
                    for j in range(TPG):
                        w = slice(j * P, (j + 1) * P)
                        mm = pe.transpose(bank[:, HB + c, w], X1[c][:, w], ident[:])
                    mm.then_inc(ms["xT"], 1)
                for c in range(n):
                    pe.wait_ge(ms["attr_copied"], nth(before, n, c))
                    for j in range(TPG):
                        w = slice(j * P, (j + 1) * P)
                        mm = pe.matmul(bank[:, U + c, w], attrT[c][:, (j // 2) * P:(j // 2 + 1) * P], wgT[:, j % 2, :], start=True, stop=True)
                    mm.then_inc(ms["g"], 1)
                for c in range(n):
                    pe.wait_ge(ms["s"], nth(before, n, c))
                    pe.matmul(bank[:, HB + c, :], ones_bf[0:3, :], bias3[:, 1, :], start=True, stop=False, skip_group_check=True)
                    for j in range(TPG):
                        w = slice(j * P, (j + 1) * P)
                        mm = pe.matmul(bank[:, HB + c, w], S[c][:, w], wT[:, 1, :], start=False, stop=True, skip_group_check=True)
                    mm.then_inc(ms["lin"], 1)

            PE_OPS = in_turn(PE_STEPS)

            def pe_window(w, kind, uses):
                for _, op, c, lag in PE_OPS:
                    of, use = group_kind(w, c, lag, kind, uses), w - lag
                    if of is None:
                        continue
                    if op == "xT":
                        pe.wait_ge(dve_front[c], after(DVE_FRONT, use, "x1"))
                        if later(use):
                            pe.wait_ge(act_done[c], after(ACT_STEPS, use - 1, "norm"))
                        for j in range(TPG):
                            cw = slice(j * P, (j + 1) * P)
                            mm = pe.transpose(bank[:, HB + c, cw], X1[c][:, cw], ident[:])
                        mm.then_inc(pe_done[c], 1)
                    elif op == ("lin", 0):
                        pe.wait_ge(act_done[c], after(ACT_STEPS, use, "ln s"))
                        pe.matmul(bank[:, U + c, :], wT[:, 0, :], S[c], start=True, stop=True, skip_group_check=True).then_inc(pe_done[c], 1)
                    elif op == "y":
                        pe.wait_ge(dve_done[c], after(DVE_STEPS, use, ("max", NSTEP - 1)))
                        pe.matmul(bank[:, HB + c, :], ones_bf[0:3, :], bias3[:, 0, :], start=True, stop=False, skip_group_check=True)
                        pe.matmul(bank[:, HB + c, :], ident[:], X1[c], start=False, stop=False, skip_group_check=True)
                        for j in range(TPG):
                            cw = slice(j * P, (j + 1) * P)
                            pe.matmul(bank[:, HB + c, cw], S[c][:, cw], gate_diag[:], start=False, stop=False, skip_group_check=True)
                            mm = pe.matmul(bank[:, HB + c, cw], H[c][:, cw], wT[:, 2, :], start=False, stop=True, skip_group_check=True)
                        mm.then_inc(pe_done[c], 1)
                    else:
                        bank0, _, w_at = STEPS[op[1]]
                        pe.wait_ge(dve_done[c], after(DVE_STEPS, use, ("max", op[1])))
                        pe.matmul(bank[:, (HB if bank0 == U else U) + c, :], wT[:, w_at, :], H[c],
                                  start=(bank0 == U), stop=True, skip_group_check=True).then_inc(pe_done[c], 1)

            def pe_messages():
                for c in range(CHAINS):
                    pe.wait_ge(act_done[c], after(ACT_STEPS, MSG_USE - 1, "norm"))
                each_run(pe, msg_runs, pe_msg)
                pe.wait_ge(ms["msg"], EG)

            pe.wait_ge(bias_ready, 96)
            pe.wait_ge(place_read, ET)
            follow_plan(pe, pe_window, near, segment_products, pe_messages)

        @block.vector
        def _(dve):
            links = [0]

            def link(ins):
                links[0] += 1
                ins.then_inc(link_sem, 1)
                dve.wait_ge(link_sem, links[0])

            dve.memset(wg_nat, 0.0).then_inc(wg_zeroed, 1)
            dve.memset(zero_row, 0.0)
            dve.memset(ones[:], 1.0)
            dve.memset(ones_bf[:], 1.0)
            dve.memset(zeros_w[:], 0.0)
            dve.memset(zeros_r[:], 0.0)
            dve.memset(src_s[:, ET:ET + 1], -1.0)
            dve.wait_ge(iotas, 5)
            dve.tensor_scalar(ident[:], col_minus_row[:], 0.0, None, ALU.is_equal)
            dve.tensor_scalar(below[:], col_minus_row[:], 0.0, None, ALU.is_gt)
            dve.tensor_scalar(earlier[:], col_minus_row[:], 0.0, None, ALU.is_lt)
            dve.tensor_scalar(shift_up[:], col_minus_row[:], -1.0, None, ALU.is_equal)
            link(dve.tensor_scalar(wrap[:], col_minus_row[:], float(P - 1), None, ALU.is_equal))
            dve.wait_ge(b_loaded, 16 * (4 + 2 * RES))
            link(dve.tensor_scalar(gate_diag[:], ident[:], cols[:, C_GATE:C_GATE + 1], None, ALU.mult))
            link(dve.tensor_copy(cols[:, C_SUM:C_SUM + 1], cols[:, C_B2:C_B2 + 1]))
            for k in range(1, RES):
                link(dve.tensor_tensor(cols[:, C_SUM + k:C_SUM + k + 1], cols[:, C_SUM + k - 1:C_SUM + k], cols[:, C_B2 + k:C_B2 + k + 1], ALU.add))
            dve.memset(tick[:], 0.0).then_inc(consts, 1)
            for part in range(3):
                link(dve.tensor_copy(bpart[:, :, part, 0, :], brow[:, :, part, :]))
                if part < 2:
                    link(dve.tensor_tensor(brow[:, :, part + 1, :], brow[:, :, part, :], bpart[:, :, part, 0, :], ALU.subtract))
                for r in range(1, TPG):
                    last = dve.tensor_copy(bpart[:, :, part, r, :], bpart[:, :, part, 0, :])
            last.then_inc(bias_parts, 1)

            dve.wait_ge(rows_loaded, 96)
            dve.tensor_copy(rows_f[:, 0, :], rows_nat[:, 0, :])
            dve.tensor_copy(rows_f[:, 3, :], rows_nat[:, 1, :])
            dve.tensor_scalar(rows_i[:, 0, :], rows_nat[:, 0, :], 8, None, ALU.logical_shift_right)
            link(dve.tensor_scalar(rows_i[:, 1, :], rows_nat[:, 0, :], DIG - 1, None, ALU.bitwise_and))
            dve.tensor_copy(rows_f[:, 1:3, :], rows_i[:, :, :]).then_inc(rows_split, 1)
            dve.wait_ge(cols_psum, 1)
            dve.tensor_copy(e_cols[:, 0:4, :], bank[:, 4, :].rearrange("p (q t) -> p q t", q=4)[:, :, 0:ET])
            link(dve.tensor_copy(e_cols[:, 4, :], bank[:, 5, 0:ET]))
            dve.tensor_copy(dst_idx, e_cols[:, 3, :]).then_inc(idx_ready, 1)
            def count_onehots(g, s):
                if not isinstance(g, int):
                    dve.wait_ge(hist_added, (g - 1) * TPG)
                for j in range(TPG):
                    t = bass.ds(g * TPG + j, 1)
                    dve.tensor_scalar(oh_hi[s][j], digits, e_cols[:, 1, t], None, ALU.is_equal)
                    dve.tensor_scalar(oh_lo[s][j], digits, e_cols[:, 2, t], None, ALU.is_equal).then_inc(onehot_ready, 1)

            count_onehots(0, 0)
            count_onehots(1, 1)
            by_twos(dve, 2, EG - 1, count_onehots)
            dve.wait_ge(hist_added, (EG - 2) * TPG)
            count_onehots(EG - 1, 0)
            dve.memset(zeros, 0.0)
            dve.wait_ge(hist_added, ET)
            link(dve.tensor_copy(hist, bank[:, 0, :]))
            for c in range(2):
                w = slice(c * DIG, (c + 1) * DIG)
                last = dve.tensor_tensor_scan(incl[:, w], hist[:, w], zeros, 0.0, ALU.add, ALU.add)
            last.then_inc(scan_ready, 1)
            dve.wait_ge(offs_psum, 1)
            link(dve.tensor_copy(offs, bank[:, 1, 0:2]))
            for c in range(2):
                w = slice(c * DIG, (c + 1) * DIG)
                dve.scalar_tensor_tensor(out=base[:, w], in0=incl[:, w], scalar=offs[:, c:c + 1], in1=hist[:, w], op0=ALU.add, op1=ALU.subtract)
                link(dve.tensor_scalar(ptr_f[:, w], incl[:, w], offs[:, c:c + 1], float(-1 - ZROW), ALU.add, ALU.add))
            link(dve.tensor_scalar(hist, hist, 1.0, None, ALU.min))
            link(dve.tensor_tensor(ptr_f, ptr_f, hist, ALU.mult))
            dve.tensor_scalar(ptr_i, ptr_f, float(ZROW), None, ALU.add).then_inc(ptr_ready, 1)

            dve.wait_ge(attr_loaded, 32)
            dve.wait_ge(idx_ready, 1)
            dve.tensor_copy(payload[:, :, 0], e_cols[:, 0, :])
            dve.tensor_copy(payload_i[:, :, 1], dst_idx)
            dve.tensor_copy(payload[:, :, 3], e_cols[:, 4, :]).then_inc(payload_set, 1)

            dve.wait_ge(row_bcast, 16)
            def place_onehots(g, s):
                chunk = bass.ds(g * GW, GW)
                if later(g) and not (isinstance(g, int) and g == 1):
                    dve.wait_ge(place_psum, (g - 1) * TPG)
                dve.tensor_scalar(hi_row[s], src_rows[:, chunk], 8, None, ALU.logical_shift_right).then_inc(hi_split, 1)
                dve.wait_ge(hi_split, g + 1)
                for c in range(2):
                    ins = dve.tensor_scalar(oh_hiT[s][c], hi_row[s], hi_no[:, c:c + 1], None, ALU.is_equal)
                ins.then_inc(onehotT_ready, 1)

            def tile_onehot(g, s, j):
                t = bass.ds(g * TPG + j, 1)
                dve.tensor_scalar(oh_hi[s][j], digits, e_cols[:, 1, t], None, ALU.is_equal)
                dve.tensor_scalar(oh_lo[s][j], digits, e_cols[:, 2, t], None, ALU.is_equal).then_inc(tile_onehots, 1)

            def read_places(g, s, ahead=True):
                if ahead:
                    place_onehots(g + 1, 1 - s)
                for j in range(TPG):
                    dve.scalar_tensor_tensor(out=same[j], in0=src_rows[:, bass.ds(g * GW + j * P, P)], scalar=e_cols[:, 0, bass.ds(g * TPG + j, 1)],
                                             in1=earlier[:], op0=ALU.is_equal, op1=ALU.mult, accum_out=acc_b[:, j:j + 1])
                    dve.wait_ge(place_psum, g * TPG + j + 1)
                    dve.tensor_tensor_reduce(junk[j], bank[:, 2 + j, 0:DIG], oh_lo[s][j], 1.0, 0.0, ALU.mult, ALU.add,
                                             acc_a[:, j:j + 1]).then_inc(place_read, 1)
                    if ahead:
                        tile_onehot(g + 1, 1 - s, j)
                dve.wait_ge(place_read, g * TPG + TPG)
                dve.tensor_tensor(pos[:, bass.ds(g * TPG, TPG)], acc_a, acc_b, ALU.add).then_inc(places_added, 1)
                dve.wait_ge(places_added, g + 1)

            place_onehots(0, 0)
            for j in range(TPG):
                tile_onehot(0, 0, j)
            read_places(0, 0)
            by_twos(dve, 1, EG - 2, read_places)
            read_places(EG - 2, 1)
            read_places(EG - 1, 0, ahead=False)
            dve.tensor_copy(pos_idx, pos).then_inc(pos_ready, 1)

            def near():
                dve.wait_ge(meta_loaded, 16)
                dve.tensor_copy(src_s[:, 0:ET], meta[:, :, 0]).then_inc(meta_split, 1)
                dve.wait_ge(near_psum, 1)
                dve.tensor_copy(srcT[0:ET, :], bank[0:ET, U, 0:P]).then_inc(srcT_ready, 1)
                dve.tensor_copy(tile_before, below[:])
                link(dve.tensor_tensor(same_next, src_s[:, 0:ET], bank[:, HB, P:P + ET], ALU.is_equal))
                dve.memset(tick[:], 0.0).then_inc(near_read, 1)
                link(dve.scalar_tensor_tensor(out=pos, in0=same_next, scalar=FAR, in1=src_s[:, 0:ET], op0=ALU.mult, op1=ALU.add))
                dve.tensor_copy(out_idx[:], pos)
                link(dve.tensor_scalar(same_next, src_s[:, 0:ET], float(N - 1), None, ALU.min))
                link(dve.tensor_copy(meta_i[:, :, 0], same_next))
                dve.wait_ge(srow_loaded, 16)
                with dve.Fori(0, EG) as g:
                    four = bass.ds(g * TPG, TPG)
                    group = bass.ds(g * GW, GW)
                    dve.tensor_tensor(seg_mask[:, group].rearrange("p (j e) -> p j e", e=P), row_buf[:, group].rearrange("p (j e) -> p j e", e=P),
                                      src_s[:, four].unsqueeze(2).to_broadcast([P, TPG, P]), ALU.is_equal)
                    dve.scalar_tensor_tensor(out=open_mask[:, group].rearrange("p (j e) -> p j e", e=P), in0=row_buf[0:ET, group].rearrange("p (j e) -> p j e", e=P),
                                             scalar=srcT[0:ET, P - 1:P], in1=tile_before[0:ET, four].unsqueeze(2).to_broadcast([ET, TPG, P]),
                                             op0=ALU.is_equal, op1=ALU.mult).then_inc(masks_ready, 1)
                dve.wait_ge(masks_ready, EG)

            def dve_scale(to, mask, weight):
                return dve.tensor_copy(to, mask) if weight is None else dve.tensor_scalar(to, mask, weight, None, ALU.mult)

            def segment_sums(k):
                if k in (1, 2):
                    dve.wait_ge(tot_gathered[k - 1], 16 * ET)

                def prepare(g, s):
                    group = bass.ds(g * GW, GW)
                    if k in (1, 2):
                        dve.tensor_tensor(G[:, group], row_buf[:, group], G[:, group], ALU.add).then_inc(seg_in, 1)
                    elif k == 3:
                        for h in range(2):
                            dve.wait_ge(seg_mm[h], g + EG * 2 * k)
                            dve.tensor_copy(seg_m[:, 2 * h * P:2 * (h + 1) * P], G[:, half(g, h)]).then_inc(seg_in, 1)
                    expand(dve, dve_scale, k, g, s, 1)

                def take(g):
                    if k < 3:
                        dve.wait_ge(seg_mm[1], g + (EG * 2 * k + 1))
                        dve.tensor_copy(G[:, half(g, 1)], bank[:, SEG_BANK[1], 0:2 * P]).then_inc(seg_taken[1], 1)

                ahead_by_one(dve, prepare, take)
                if k == 3:
                    for h in range(2):
                        dve.wait_ge(seg_taken[h], EG * (2 * k + 1))
                    dve.tensor_copy(seg_m[:, 0:ET], G[:].rearrange("p (t e) -> p t e", e=P)[:, :, P - 1]).then_inc(open_copied, 1)
                    dve.wait_ge(open_T, 1)
                    link(dve.tensor_copy(open_sums, bank[0:ET, U, 0:P]))
                else:
                    dve.wait_ge(open_loaded, 16 * (k + 1))
                for part in range(3):
                    split = dve.tensor_copy(open_parts[:, part, :], open_sums)
                    if part < 2:
                        link(split)
                        link(dve.tensor_tensor(open_sums, open_sums, open_parts[:, part, :], ALU.subtract))
                split.then_inc(open_split, 1)
                with dve.Fori(0, EG) as g:
                    for h in range(2):
                        dve.wait_ge(seg_mm[h], g + (EG * (2 * k + 1) + 1))
                        dve.tensor_tensor(G[:, half(g, h)], bank[:, SEG_BANK[h], 0:2 * P], G[:, half(g, h)], ALU.add).then_inc(seg_taken[h], 1)

            def row_stats(c, k, rows):
                for j in range(TPG):
                    last = dve.bn_stats(stats[c][k][:, j, :], rows[:, j * P:(j + 1) * P])
                return last

            def row_means(c, k):
                for j in range(TPG):
                    last = dve.bn_aggr(mv[c][:, k, j, :], stats[c][k][:, j, :])
                return last

            def row_vars(c, k):
                return dve.tensor_scalar(ve[c][:, k, :], mv[c][:, k, :, 1], EPS if k else EPS / 4, None, ALU.add)

            def row_norms(c):
                for j in range(TPG):
                    w = slice(j * P, (j + 1) * P)
                    last = dve.tensor_scalar(X1[c][:, w], X[c][:, w], mv[c][:, 0, j, 0:1], rs[c][:, 0, j:j + 1], ALU.subtract, ALU.mult)
                return last

            def msg_norm(n, grp, before):
                if later(before):
                    dve.wait_ge(ms["x1"], before)
                for c in range(n):
                    rows = bass.ds((grp + c) * GW, GW)
                    dve.scalar_tensor_tensor(out=X[c], in0=G[:, rows], scalar=0.5, in1=row_buf[:, rows], op0=ALU.mult, op1=ALU.add).then_inc(ms["v"], 1)
                for c in range(n):
                    dve.wait_ge(ms["v"], nth(before, n, c))
                    row_stats(c, 0, X[c]).then_inc(ms["stats"], 1)
                dve.wait_ge(ms["stats"], nth(before, n, n - 1))
                dve.memset(tick[:], 0.0)
                for c in range(n):
                    row_means(c, 0).then_inc(ms["mean"], 1)
                for c in range(n):
                    dve.wait_ge(ms["mean"], nth(before, n, c))
                    row_vars(c, 0).then_inc(ms["var"], 1)
                if later(before):
                    dve.wait_ge(ms["xT"], before)
                for c in range(n):
                    dve.wait_ge(ms["rstd"], nth(before, n, c))
                    row_norms(c).then_inc(ms["x1"], 1)

            def msg_gate(n, grp, before):
                dve.wait_ge(ms["g"], nth(before, n, n - 1))
                for c in range(n):
                    dve.wait_ge(ms["exp"], nth(before, n, c))
                    dve.tensor_scalar(EL[c], EL[c], CAP, None, ALU.min).then_inc(ms["capped"], 1)
                for c in range(n):
                    dve.wait_ge(ms["log"], nth(before, n, c))
                    dve.tensor_tensor(H[c], bank[:, HB + c, :], EL[c], ALU.max).then_inc(ms["sp"], 1)
                for c in range(n):
                    dve.wait_ge(ms["sp"], nth(before, n, c))
                    dve.tensor_tensor(G[:, bass.ds((grp + c) * GW, GW)], bank[:, U + c, :], H[c], ALU.mult).then_inc(ms["msg"], 1)

            DVE_OPS = in_turn(["v"] + DVE_FRONT + DVE_STEPS)

            def dve_window(w, kind, uses):
                for _, op, c, lag in DVE_OPS:
                    of, use = group_kind(w, c, lag, kind, uses), w - lag
                    if of is None:
                        continue
                    edge_rows = None if of == "node" else bass.ds((use * CHAINS + c - NG) * GW, GW)
                    if op == "v":
                        if of == "edge":
                            dve.wait_ge(x_arrived[c], (use + 1) * 16)
                            if isinstance(use, int) and use * CHAINS + c == NG:
                                dve.wait_ge(xs_gathered, 16 * ET)
                                for h in range(2):
                                    dve.wait_ge(seg_taken[h], 2 * EG * 4)
                            dve.scalar_tensor_tensor(out=X[c], in0=X[c], scalar=0.5, in1=row_buf[:, edge_rows],
                                                     op0=ALU.mult, op1=ALU.add).then_inc(edge_v, 1)
                    elif op == "stats 1":
                        if of == "edge":
                            dve.wait_ge(edge_v, use * CHAINS + (c - NG + 1))
                        else:
                            dve.wait_ge(x_arrived[c], (use + 1) * 16)
                        row_stats(c, 0, X[c]).then_inc(dve_front[c], 1)
                    elif op == "mean 1":
                        dve.wait_ge(dve_front[c], after(DVE_FRONT, use, "stats 1"))
                        dve.memset(tick[:], 0.0)
                        row_means(c, 0).then_inc(dve_front[c], 1)
                    elif op == "var 1":
                        dve.wait_ge(dve_front[c], after(DVE_FRONT, use, "mean 1"))
                        row_vars(c, 0).then_inc(dve_front[c], 1)
                    elif op == "x1":
                        dve.wait_ge(pool_front[c], after(POOL_FRONT, use, "rstd 1"))
                        if later(use):
                            dve.wait_ge(pe_done[c], after(PE_STEPS, use - 1, "y"))
                        row_norms(c).then_inc(dve_front[c], 1)
                    elif op == "stats 2":
                        dve.wait_ge(pe_done[c], after(PE_STEPS, use, "y"))
                        row_stats(c, 1, bank[:, HB + c, :]).then_inc(dve_done[c], 1)
                    elif op == "mean 2":
                        dve.wait_ge(dve_done[c], after(DVE_STEPS, use, "stats 2"))
                        dve.memset(tick[:], 0.0)
                        row_means(c, 1).then_inc(dve_done[c], 1)
                    elif op == "var 2":
                        dve.wait_ge(dve_done[c], after(DVE_STEPS, use, "mean 2"))
                        row_vars(c, 1).then_inc(dve_done[c], 1)
                    elif op == "nmean":
                        dve.wait_ge(pool_done[c], after(POOL_STEPS, use, "rstd 2"))
                        dve.scalar_tensor_tensor(out=nm[c][:], in0=mv[c][:, 1, :, 0], scalar=-1.0, in1=rs[c][:, 1, :],
                                                 op0=ALU.mult, op1=ALU.mult).then_inc(dve_done[c], 1)
                    elif op[0] == "cap":
                        dve.wait_ge(act_done[c], after(ACT_STEPS, use, ("exp", op[1])))
                        dve.tensor_scalar(EL[c], EL[c], CAP, None, ALU.min).then_inc(dve_done[c], 1)
                    else:
                        k = op[1]
                        bank0, bias, _ = STEPS[k]
                        if k == (of == "node") and later(use):
                            stored = use * 16 if of == "node" else (use - NODE_USES[c]) * (16 * TPG) + 16 * NODE_USES[c]
                            dve.wait_ge(out_stored[c], stored)
                        dve.wait_ge(act_done[c], after(ACT_STEPS, use, ("ln", k)))
                        to = bank[:, U + c, :] if k == 0 and of == "node" else H[c]
                        done = edge_u0 if k == 0 and of == "edge" else dve_done[c]
                        if bias is None:
                            dve.tensor_tensor(to, bank[:, bank0 + c, :], EL[c], ALU.max).then_inc(done, 1)
                        else:
                            dve.scalar_tensor_tensor(out=to, in0=bank[:, bank0 + c, :], scalar=cols[:, bias:bias + 1], in1=EL[c],
                                                     op0=ALU.add, op1=ALU.max).then_inc(done, 1)
                        if k == 0 and of == "edge":
                            dve.wait_ge(edge_u0, use * CHAINS + (c - NG + 1))
                            dve.tensor_tensor(bank[:, U + c, :], H[c], G[:, edge_rows], ALU.add).then_inc(dve_done[c], 1)

            def dve_messages():
                dve.wait_ge(tot_gathered[2], 16 * ET)
                for _, reps, n, first, before, _ in msg_runs:
                    msg_norm(n, first, before)
                    if reps > 1:
                        with dve.Fori(0, reps - 1) as g:
                            msg_norm(n, (g + 1) * n + first, (g + 1) * n + before)
                            msg_gate(n, g * n + first, g * n + before)
                    done = (reps - 1) * n
                    msg_gate(n, first + done, before + done)
                dve.wait_ge(ms["msg"], EG)

            follow_plan(dve, dve_window, near, segment_sums, dve_messages)


_INS = ["x", "src", "dst", "edge_attr_64", "edge_weight", "L1_gnn_Wg", "L1_gnn_Wi", "L1_gnn_bi", "L1_gnn_Wj", "L1_gnn_bj",
        "L1_gnn_Wv", "L1_gnn_bv", "L1_gnn_gate", "L1_gnn_res_W1", "L1_gnn_res_b1", "L1_gnn_res_W2", "L1_gnn_res_b2"]


def kernel(**inputs):
    import numpy as _np
    import concourse.bacc as _bacc
    from concourse import mybir as _mybir
    from concourse.bass_utils import run_bass_kernel_spmd as _run

    nc = _bacc.Bacc("TRN2", target_bir_lowering=False, num_devices=1)
    arrays, args = {}, []
    for name in _INS:
        a = _np.ascontiguousarray(inputs[name])
        arrays[f"in_{name}"] = a
        args.append(nc.dram_tensor(f"in_{name}", a.shape, _mybir.dt.from_np(a.dtype), kind="ExternalInput").ap())
    out = nc.dram_tensor("out_0", arrays["in_x"].shape, _mybir.dt.float32, kind="ExternalOutput").ap()
    gnn_kernel(nc, *args, out)
    r = _run(nc, [arrays], core_ids=[0])
    return r.results[0]["out_0"]
```
